# Optimizing a Trainium2 kernel written in Bass

```python
import numpy as np
import jax
import jax.numpy as jnp

def _softmax(x, axis=-1):
    return jax.nn.softmax(x, axis=axis)

def _gelu(x):
    return jax.nn.gelu(x, approximate=True)

def _silu(x):
    return jax.nn.silu(x)

def _sigmoid(x):
    return jax.nn.sigmoid(x)

def _layernorm(x, axis=-1, eps=1e-05):
    m = jnp.mean(x, axis=axis, keepdims=True)
    v = jnp.var(x, axis=axis, keepdims=True)
    return (x - m) / jnp.sqrt(v + eps)

def _scatter_add(tgt, idx, src, axis=0):
    return tgt.at[idx].add(src)

def _segment_sum(src, seg, n):
    return jax.ops.segment_sum(src, seg, n)
kernel_name = 'mk_adj_preln_d4_adj_r2_2ba728'

def setup_inputs(seed: int=0):
    np.random.seed(seed)
    _w = jnp.asarray

    def _rec_inputs():
        import jax
        import jax.numpy as jnp
        _gk = jax.random.key(seed)
        x = -0.0005207 + 1.001 * jax.random.normal(jax.random.fold_in(_gk, 1), (4096, 128), jnp.float32)
        _a = jax.random.bernoulli(jax.random.fold_in(_gk, 2), 0.00390625, (4096, 4096))
        _a = jnp.logical_or(_a, jnp.eye(4096, dtype=bool))
        _af = _a.astype(jnp.float32)
        _af = _af * jax.random.uniform(jax.random.fold_in(_gk, 3), (4096, 4096), jnp.float32, 0.05, 1)
        adj = _af
        return (x, adj)
    x, adj = _rec_inputs()

    def _L0_gnn_setup():
        import jax, jax.numpy as jnp
        import numpy as np
        N = 8192
        IN_DIM = 128
        OUT_DIM = 128

        def _message(X, A, W):
            deg = jnp.sum(A, axis=1, keepdims=True)
            A_norm = A / jnp.where(deg > 0, deg, 1.0)
            return A_norm @ X @ W
        key = jax.random.key(seed)
        k1, k2, k3, k4 = jax.random.split(key, 4)
        X = jax.random.normal(k1, (N, IN_DIM), dtype=jnp.float32)
        A = jax.random.uniform(k2, (N, N), dtype=jnp.float32)
        W_in = jax.random.normal(k3, (IN_DIM, OUT_DIM), dtype=jnp.float32) / np.sqrt(IN_DIM)
        W_out = jax.random.normal(k4, (IN_DIM, OUT_DIM), dtype=jnp.float32) / np.sqrt(IN_DIM)
        return {'X': X, 'A': A, 'W_in': W_in, 'W_out': W_out}
    _L0_gnn_all = _L0_gnn_setup()
    _L0_gnn_in = {k: v for k, v in _L0_gnn_all.items() if k in ('W_in', 'W_out')}
    del _L0_gnn_all

    def _L1_gnn_setup():
        import jax, jax.numpy as jnp
        import numpy as np
        N = 8192
        U = 128
        AVG_DEGREE = 32
        key = jax.random.key(seed)
        kx, ka, kw = jax.random.split(key, 3)
        x = jax.random.normal(kx, (N, U), dtype=jnp.float32)
        adj = (jax.random.uniform(ka, (N, N)) < AVG_DEGREE / N).astype(jnp.float32)
        W = jax.random.normal(kw, (U, U), dtype=jnp.float32) * 0.05
        b = jnp.zeros((U,), dtype=jnp.float32)
        return {'x': x, 'adj': adj, 'W': W, 'b': b}
    _L1_gnn_all = _L1_gnn_setup()
    _L1_gnn_in = {k: v for k, v in _L1_gnn_all.items() if k in ('W', 'b')}
    del _L1_gnn_all

    def _L2_gnn_setup():
        import jax, jax.numpy as jnp
        import numpy as np
        N = 4096
        F = 128
        U = 128
        EDGE_P = 0.002

        def adj_norm(adj):
            a_hat = adj + jnp.eye(adj.shape[0], dtype=adj.dtype)
            d_inv_sqrt = jax.lax.rsqrt(jnp.sum(a_hat, axis=-1))
            return a_hat * d_inv_sqrt[:, None] * d_inv_sqrt[None, :]
        key = jax.random.key(seed)
        k1, k2, k3 = jax.random.split(key, 3)
        a = (jax.random.uniform(k1, (N, N)) < EDGE_P).astype(jnp.float32)
        adj = jnp.maximum(a, a.T)
        x = jax.random.normal(k2, (N, F), dtype=jnp.float32)
        W = jax.random.normal(k3, (F, U), dtype=jnp.float32) * 0.05
        b = jnp.zeros((U,), dtype=jnp.float32)
        return {'x': x, 'adj': adj, 'W': W, 'b': b}
    _L2_gnn_all = _L2_gnn_setup()
    _L2_gnn_in = {k: v for k, v in _L2_gnn_all.items() if k in ('W', 'b')}
    del _L2_gnn_all

    def _L3_gnn_setup():
        import jax, jax.numpy as jnp
        import numpy as np
        N = 8192
        C = 128
        F = 128
        key = jax.random.key(seed)
        k1, k2, k3, k4 = jax.random.split(key, 4)
        X = jax.random.normal(k1, (N, C), dtype=jnp.float32)
        adj = jax.random.uniform(k2, (N, N), dtype=jnp.float32)
        W = jax.random.normal(k3, (C, F), dtype=jnp.float32) * 0.05
        b = jax.random.normal(k4, (F,), dtype=jnp.float32) * 0.05
        return {'X': X, 'adj': adj, 'W': W, 'b': b}
    _L3_gnn_all = _L3_gnn_setup()
    _L3_gnn_in = {k: v for k, v in _L3_gnn_all.items() if k in ('W', 'b')}
    del _L3_gnn_all
    return {'x': x, 'adj': adj, 'L0_gnn_W_in': _L0_gnn_in['W_in'], 'L0_gnn_W_out': _L0_gnn_in['W_out'], 'L1_gnn_W': _L1_gnn_in['W'], 'L1_gnn_b': _L1_gnn_in['b'], 'L2_gnn_W': _L2_gnn_in['W'], 'L2_gnn_b': _L2_gnn_in['b'], 'L3_gnn_W': _L3_gnn_in['W'], 'L3_gnn_b': _L3_gnn_in['b']}

def reference(x, adj, L0_gnn_W_in, L0_gnn_W_out, L1_gnn_W, L1_gnn_b, L2_gnn_W, L2_gnn_b, L3_gnn_W, L3_gnn_b):
    import jax
    import jax.numpy as jnp

    def _L0_gnn_ref(X, A, W_in, W_out):
        import jax, jax.numpy as jnp
        import numpy as np
        N = 8192
        IN_DIM = 128
        OUT_DIM = 128

        def _message(X, A, W):
            deg = jnp.sum(A, axis=1, keepdims=True)
            A_norm = A / jnp.where(deg > 0, deg, 1.0)
            return A_norm @ X @ W
        X_in = _message(X, A, W_in)
        X_out = _message(X, A.T, W_out)
        return X_in + X_out

    def _L1_gnn_ref(x, adj, W, b):
        import jax, jax.numpy as jnp
        import numpy as np
        N = 8192
        U = 128
        AVG_DEGREE = 32
        adj = jax.lax.stop_gradient(adj)
        neigh1 = adj @ x
        x1 = jax.nn.swish(neigh1 @ W + b)
        neigh2 = adj @ x1
        x2 = jax.nn.swish(neigh2 @ W + b)
        return x2

    def _L2_gnn_ref(x, adj, W, b):
        import jax, jax.numpy as jnp
        import numpy as np
        N = 4096
        F = 128
        U = 128
        EDGE_P = 0.002

        def adj_norm(adj):
            a_hat = adj + jnp.eye(adj.shape[0], dtype=adj.dtype)
            d_inv_sqrt = jax.lax.rsqrt(jnp.sum(a_hat, axis=-1))
            return a_hat * d_inv_sqrt[:, None] * d_inv_sqrt[None, :]
        adj_n = adj_norm(adj)
        h = adj_n @ x
        h = h @ W + b
        return jax.nn.relu(h)

    def _L3_gnn_ref(X, adj, W, b):
        import jax, jax.numpy as jnp
        import numpy as np
        N = 8192
        C = 128
        F = 128
        adj_hat = adj + jnp.eye(adj.shape[0], dtype=adj.dtype)
        d_inv_sqrt = 1.0 / jnp.sqrt(jnp.sum(adj_hat, axis=1))
        adj_norm = adj_hat * d_inv_sqrt[:, None] * d_inv_sqrt[None, :]
        out = adj_norm @ (X @ W) + b
        return jax.nn.relu(out)
    h = jnp.maximum(_layernorm(x, axis=-1), 0.0)
    x = x + _L0_gnn_ref(h, adj, L0_gnn_W_in, L0_gnn_W_out)
    h = jnp.maximum(_layernorm(x, axis=-1), 0.0)
    x = x + _L1_gnn_ref(h, adj, L1_gnn_W, L1_gnn_b)
    h = jnp.maximum(_layernorm(x, axis=-1), 0.0)
    x = x + _L2_gnn_ref(h, adj, L2_gnn_W, L2_gnn_b)
    h = jnp.maximum(_layernorm(x, axis=-1), 0.0)
    x = x + _L3_gnn_ref(h, adj, L3_gnn_W, L3_gnn_b)
    return x

_drawn_inputs = setup_inputs


def setup_inputs(seed=0):
    import zlib

    import numpy as np

    out = dict(_drawn_inputs(seed))
    spreads = {'L1_gnn_b': (0.0, 0.1), 'L2_gnn_b': (0.0, 0.531)}
    factors = {'L3_gnn_b': 7.403}
    for name, (base, spread) in spreads.items():
        noise = np.random.default_rng([zlib.crc32(name.encode()), seed]).standard_normal(out[name].shape)
        drawn = base * np.exp(spread * noise) if base else spread * noise
        out[name] = jnp.asarray(drawn.astype(out[name].dtype))
    for name, factor in factors.items():
        out[name] = (out[name] * factor).astype(out[name].dtype)
    return out
```

```python
from contextlib import ExitStack

import concourse.bass as bass
from concourse import mybir

F32 = mybir.dt.float32
F32R = mybir.dt.float32r
ALU = mybir.AluOpType
ACT = mybir.ActivationFunctionType
AX_X = mybir.AxisListType.X
ds = bass.ds

P = 128
EPS = 1e-5


def build_gnn_stack(nc, x, adj, w_in, w_out, w1, b1, w2, b2, w3, b3, out):
    N, D = x.shape
    assert D == P and N % 1024 == 0
    NB = N // P
    GB = 4
    GW = GB * P
    NG = N // GW
    CB = 8
    CW = CB * P
    NCH = N // CW
    UNITS = NCH * NG
    STEPS = UNITS * CB
    SUBS = UNITS * GB
    SB2 = 2
    NS = NB // SB2
    NT = NS // 2
    SWEEPS = 4
    Z0 = 2 * NG

    adj_t = nc.dram_tensor("adj_t_scratch", (NG, P, NB * GW), F32, kind="Internal").ap()

    ctx = ExitStack()
    with ctx:
        def sb(name, shape, dt=F32):
            return ctx.enter_context(nc.sbuf_tensor(name, shape, dt))

        def sem(name):
            return ctx.enter_context(nc.semaphore(name))

        x_sb = sb("x_sb", [P, NB, D])
        h_hi = [sb(f"h_hi{i}", [P, NB, D], F32R) for i in range(2)]
        h_lo = [sb(f"h_lo{i}", [P, NB, D], F32R) for i in range(2)]
        raw = sb("raw", [P, 8, 1024])
        a_hi = sb("a_hi", [P, 6, 1024], F32R)
        a_lo = sb("a_lo", [P, 6, 1024], F32R)
        at_raw = sb("at_raw", [P, 2, GB * GW])
        acc = sb("acc", [P, N])
        prod_t = sb("prod_t", [P, 2, GW])
        w_sb = sb("w_sb", [P, 5, D])
        b_sb = sb("b_sb", [P, 3, D])
        ident = sb("ident", [P, P])
        ident_r = sb("ident_r", [P, P], F32R)
        row_part = sb("row_part", [P, NB, NCH])
        col_part = sb("col_part", [P, NB, NG])
        deg = sb("deg", [P, 4, GB])
        deg_sum = sb("deg_sum", [P, NB])
        inv_row = sb("inv_row", [P, NB])
        inv_col = sb("inv_col", [P, NB])
        d_isqrt = sb("d_isqrt", [P, NB])
        zt = sb("zt", [P, GW])
        act_raw = sb("act_raw", [P, GW])
        stats = sb("stats", [P, GB, 6])
        mv = sb("mv", [P, GB, 2])
        std = sb("std", [P, GB])
        rstd = sb("rstd", [P, GB])
        lnscale = sb("lnscale", [P, GB])
        lnbias = sb("lnbias", [P, GB])
        carrier = sb("carrier", [P, 1])
        eps_sb = sb("eps_sb", [P, 1])
        one_sb = sb("one_sb", [P, 1])

        banks = [ctx.enter_context(nc.psum_tensor(f"bank{i}", [P, 512], F32)) for i in range(8)]
        turn_ps, row_ps, col_ps, z_ps = banks[0:2], banks[2:4], banks[4:6], banks[6:8]
        prod_ps = banks[0:2]

        hc_hi, hc_lo = h_hi[1][:, NB - CB:NB, :], h_lo[1][:, NB - CB:NB, :]
        hd_hi = a_hi[:, 4, 0:GW].rearrange("p (b f) -> p b f", b=GB)
        hd_lo = a_lo[:, 4, 0:GW].rearrange("p (b f) -> p b f", b=GB)

        def nat_raw(u, a):
            return raw[:, 4 * (u % 2) + a, :]

        def nat(t, a):
            return t[:, a, :]

        def atb(t, k):
            k = k % 4
            return t[:, 4 + k // 2, (k % 2) * GW:(k % 2 + 1) * GW]

        def sub_raw(s):
            return raw[:, s % 8, :]

        def sub(t, s):
            return t[:, s % 4, :]

        x_in = [sem(f"x_in{g}") for g in range(2)]
        const_in = sem("const_in")
        ident_made = sem("ident_made")
        ones_made = sem("ones_made")
        nat_in = [sem(f"nat_in{i}") for i in range(8)]
        tile_in = [sem(f"tile_in{i}") for i in range(4)]
        stored = [sem(f"stored{i}") for i in range(2)]
        turned = sem("turned")
        at_raw_done = sem("at_raw_done")
        at_hi_done = sem("at_hi_done")
        turn_free = sem("turn_free")
        at_lo_done = sem("at_lo_done")
        at_free = sem("at_free")
        nat_hi_done = sem("nat_hi_done")
        nat_lo_done = sem("nat_lo_done")
        nat_free = sem("nat_free")
        row_free = sem("row_free")
        col_free = sem("col_free")
        hc_ready = sem("hc_ready")
        acc_clear = sem("acc_clear")
        z_ready = sem("z_ready")
        z_free = sem("z_free")
        sub_hi = sem("sub_hi")
        sub_lo = sem("sub_lo")
        sub_used = sem("sub_used")
        prod_free = sem("prod_free")
        hd_ready = sem("hd_ready")
        zt_ready = sem("zt_ready")
        silu_ready = sem("silu_ready")
        x_upd = sem("x_upd")
        stats_ready = sem("stats_ready")
        mv_ready = sem("mv_ready")
        std_ready = sem("std_ready")
        rstd_ready = sem("rstd_ready")
        lnscale_ready = sem("lnscale_ready")
        lnbias_ready = sem("lnbias_ready")
        act_ready = sem("act_ready")
        h_hi_ready = sem("h_hi_ready")
        h_ready = sem("h_ready")
        deg_step = sem("deg_step")
        dsq_ready = sem("dsq_ready")
        out_done = sem("out_done")

        LN_BEFORE = {-1: 0, 0: NG, 2: 2 * NG, 3: 3 * NG}
        SPLIT_BEFORE = {-1: 0, 0: NG, 1: 2 * NG, 2: 3 * NG, 3: 4 * NG}
        XUPD_BEFORE = {2: 0, 3: NG, 4: 2 * NG}
        ZT_BEFORE = {1: 0, 2: NG, 3: 2 * NG, 4: 3 * NG}
        SET_OF = {-1: 0, 0: 1, 1: 0, 2: 1, 3: 0}
        W_OF = {1: 2, 2: 2, 3: 3, 4: 4}
        B_OF = {1: 0, 2: 0, 3: 1, 4: 2}

        DEG_COL = 5 * 2
        DEG_ROW = 5
        DEG_ALL = NCH * DEG_COL + NG * DEG_ROW + 2

        def run_groups(eng, sweep, group):
            group(sweep, 0, 0)
            with eng.Fori(0, (NG - 2) // 2) as m:
                group(sweep, 2 * m + 1, 1)
                group(sweep, 2 * m + 2, 0)
            group(sweep, NG - 1, 1)

        def before(sweep, q):
            if isinstance(q, int) and q == 0:
                return sweep - 1, NG - 1
            return sweep, q - 1

        block = ctx.enter_context(nc.Block())

        @block.sync
        def _(sp):
            xv = x.rearrange("(b p) d -> p b d", p=P)
            for g in range(2):
                sp.dma_start(x_sb[:, g * NB // 2:(g + 1) * NB // 2, :],
                             xv[:, g * NB // 2:(g + 1) * NB // 2, :]).then_inc(x_in[g], 16)

            def load_nat(c, g):
                for a in range(GB):
                    sp.dma_start(nat_raw(g, a), adj[(GB * g + a) * P:(GB * g + a + 1) * P, ds(c * CW, CW)])\
                      .then_inc(nat_in[4 * (g % 2) + a], 16)

            load_nat(0, 0)
            for i, w in enumerate((w_in, w_out, w1, w2, w3)):
                sp.dma_start(w_sb[:, i, :], w).then_inc(const_in, 16)
            for i, b in enumerate((b1, b2, b3)):
                sp.dma_start(b_sb[:, i, :], b.rearrange("(a n) -> a n", a=1).to_broadcast([P, D])).then_inc(const_in, 16)
            load_nat(0, 1)

            def store(c, g, half):
                s = 2 * g + half
                sp.wait_ge(at_raw_done, c * NG * CB + g * CB + 4 * half + 4)
                sp.dma_start(adj_t[g, :, ds(c * CB * GW + half * 4 * GW, 4 * GW)], at_raw[:, s % 2, :])\
                  .then_inc(stored[s % 2], 16)

            def sweep0(c, last):
                for g in range(NG):
                    store(c, g, 0)
                    if not (last and g >= NG - 2):
                        sp.wait_ge(turned, (c * NG + g) * CB + CB)
                        sp.wait_ge(nat_lo_done, (c * NG + g) * GB + GB)
                        load_nat(c + (g + 2) // NG, (g + 2) % NG)
                    store(c, g, 1)

            with sp.Fori(0, NCH - 1) as c:
                sweep0(c, False)
            sweep0(NCH - 1, True)
            for s in range(2):
                sp.wait_ge(stored[s], 16 * UNITS)

            sp.wait_ge(turned, STEPS)
            sp.wait_ge(nat_lo_done, SUBS)

            def load_tiles(sweep, q):
                for t in range(NT):
                    tile = ((sweep - 1) * NG + q) * NT + t
                    if not (sweep == 1 and isinstance(q, int) and t < 4):
                        sp.wait_ge(sub_lo, 2 * tile - 6)
                    sp.dma_start(raw[:, 2 * (t % 4):2 * (t % 4) + 2, :].rearrange("p a n -> p (a n)"),
                                 adj_t[q, :, t * 2048:(t + 1) * 2048]).then_inc(tile_in[t % 4], 16)

            load_tiles(1, 0)
            with sp.Fori(1, NG) as q:
                load_tiles(1, q)
            for sweep in range(2, SWEEPS + 1):
                with sp.Fori(0, NG) as q:
                    load_tiles(sweep, q)

            with sp.Fori(0, NG) as q:
                sp.wait_ge(x_upd, XUPD_BEFORE[4] + q + 1)
                sp.dma_start(out.rearrange("(g b p) d -> g p b d", p=P, b=GB)[q], x_sb[:, ds(GB * q, GB), :])\
                  .then_inc(out_done, 16)
            sp.wait_ge(out_done, 16 * NG)

        @block.gpsimd
        def _(pool):
            pool.memset(ident[:, :], 0.0).then_inc(ident_made, 1)
            pool.memset(eps_sb[:, :], EPS).then_inc(ones_made, 1)
            pool.memset(one_sb[:, :], 1.0).then_inc(ones_made, 1)
            pool.wait_ge(ident_made, 1)
            pool.affine_select(out=ident[:, :], in_=ident[:, :], compare_op=ALU.not_equal, fill=1.0,
                               base=0, pattern=[[-1, P]], channel_multiplier=1).then_inc(ident_made, 1)

            def split_lo(sweep, q):
                s = SET_OF[sweep]
                pool.wait_ge(h_hi_ready, SPLIT_BEFORE[sweep] + q + 1)
                pool.tensor_tensor(h_lo[s][:, ds(GB * q, GB), :],
                                   act_raw[:, :].rearrange("p (b f) -> p b f", b=GB),
                                   h_hi[s][:, ds(GB * q, GB), :].bitcast(F32), ALU.subtract).then_inc(h_ready, 1)

            with pool.Fori(0, NG) as q:
                split_lo(-1, q)

            def nat_split(c, g, a):
                n = (c * NG + g) * GB + a
                pool.wait_ge(nat_hi_done, n + 1)
                pool.tensor_tensor(nat(a_lo, a), nat_raw(g, a), nat(a_hi, a).bitcast(F32),
                                   ALU.subtract).then_inc(nat_lo_done, 1)

            def sweep0(c, last):
                for g in range(NG):
                    for a in range(GB):
                        nat_split(c, g, a)
                        if last and a == 0 and g >= 2:
                            split_lo(0, g - 2)

            with pool.Fori(0, NCH - 1) as c:
                sweep0(c, False)
            sweep0(NCH - 1, True)
            split_lo(0, NG - 2)
            split_lo(0, NG - 1)

            def group(sweep, q, odd):
                if sweep >= 3:
                    if not (sweep == 3 and isinstance(q, int) and q == 0):
                        pool.wait_ge(sub_used, ((sweep - 1) * NG + q) * NS)
                    s = SET_OF[sweep - 1]
                    pool.wait_ge(h_ready, SPLIT_BEFORE[sweep - 1] + q + 1)
                    pool.tensor_copy(hd_hi, h_hi[s][:, ds(GB * q, GB), :].bitcast(F32)).then_inc(hd_ready, 1)
                    pool.tensor_copy(hd_lo, h_lo[s][:, ds(GB * q, GB), :].bitcast(F32)).then_inc(hd_ready, 1)
                ps, pq = before(sweep, q)
                if 1 <= ps <= 3:
                    split_lo(ps, pq)

            for sweep in range(1, SWEEPS + 1):
                run_groups(pool, sweep, group)

        @block.scalar
        def _(act):
            act.wait_ge(ident_made, 2)
            act.activation(ident_r[:, :], ident[:, :], ACT.Copy).then_inc(ident_made, 1)
            act.wait_ge(ones_made, 2)

            def ln_std(n):
                act.wait_ge(mv_ready, n + 1)
                act.activation(std[:, :], mv[:, :, 1], ACT.Sqrt, bias=eps_sb[:, 0:1]).then_inc(std_ready, 1)

            def split_hi(sweep, q):
                m = SPLIT_BEFORE[sweep] + q
                act.wait_ge(act_ready, m + 1)
                act.activation(h_hi[SET_OF[sweep]][:, ds(GB * q, GB), :],
                               act_raw[:, :].rearrange("p (b f) -> p b f", b=GB), ACT.Copy).then_inc(h_hi_ready, 1)

            def ln_relu(sweep, q):
                n, m = LN_BEFORE[sweep] + q, SPLIT_BEFORE[sweep] + q
                act.wait_ge(lnbias_ready, n + 1)
                if not (sweep == -1 and isinstance(q, int) and q == 0):
                    act.wait_ge(h_ready, m)
                for b in range(GB):
                    last = act.activation(act_raw[:, b * D:(b + 1) * D], x_sb[:, GB * q + b, :], ACT.Relu,
                                          bias=lnbias[:, b:b + 1], scale=lnscale[:, b:b + 1])
                last.then_inc(act_ready, 1)
                split_hi(sweep, q)

            for q in range(NG):
                ln_std(q)
                ln_relu(-1, q)

            def nat_hi(c, g, a):
                n = (c * NG + g) * GB + a
                act.wait_ge(nat_in[4 * (g % 2) + a], 16 * (c * (NG // 2) + g // 2) + 16)
                act.wait_ge(nat_free, n + 1)
                act.activation(nat(a_hi, a), nat_raw(g, a), ACT.Copy,
                               accum_out=row_part[:, GB * g + a, ds(c, 1)]).then_inc(nat_hi_done, 1)

            def at_hi(c, g, k):
                s = (c * NG + g) * CB + k
                act.wait_ge(turned, s + 1)
                act.wait_ge(at_free, s + 1)
                act.activation(atb(a_hi, k), turn_ps[k % 2][:, :], ACT.Copy,
                               accum_out=col_part[:, ds(CB * c + k, 1), g]).then_inc(at_hi_done, 1)

            def col_out(c):
                act.wait_ge(nat_free, 4 + (c + 1) * NG * GB)
                for half in range(2):
                    last = act.activation(prod_t[:, half, :], col_ps[half][:, :], ACT.Copy)
                last.then_inc(col_free, 1)

            def sweep0(c, last):
                for g in range(NG):
                    for k in range(CB):
                        if last and g >= 2 and k == 1:
                            ln_relu(0, g - 2)
                        at_hi(c, g, k)
                        if k % 2 == 0:
                            a = k // 2 + 2
                            if not (last and g == NG - 1 and a >= GB):
                                nat_hi(c + (g + a // GB) // NG, (g + a // GB) % NG, a % GB)
                        if last and g >= 1 and g - 1 < NG - 2 and k == CB - 1:
                            ln_std(LN_BEFORE[0] + g - 1)
                col_out(c)

            nat_hi(0, 0, 0)
            nat_hi(0, 0, 1)
            with act.Fori(0, NCH - 1) as c:
                sweep0(c, False)
            sweep0(NCH - 1, True)
            for q in (NG - 2, NG - 1):
                ln_std(LN_BEFORE[0] + q)
                ln_relu(0, q)
            act.wait_ge(deg_step, DEG_ALL)
            act.activation(d_isqrt[:, :], d_isqrt[:, :], ACT.Sqrt).then_inc(dsq_ready, 1)

            def group(sweep, q, odd):
                ps, pq = before(sweep, q)
                for s in range(NS):
                    sidx = ((sweep - 1) * NG + q) * NS + s
                    if s % 2 == 0:
                        act.wait_ge(tile_in[(s // 2) % 4], 16 * (((sweep - 1) * NG + q) * 2 + s // 8 + 1))
                    if sweep == 1 and isinstance(q, int) and q == 0 and s < 4:
                        if s == 0:
                            act.wait_ge(nat_free, 4 + SUBS)
                    else:
                        act.wait_ge(sub_used, sidx - 3)
                    act.activation(sub(a_hi, s), sub_raw(s), ACT.Copy).then_inc(sub_hi, 1)
                    if ps == 0:
                        continue
                    if s == 3:
                        prod_out(ps, pq, 1 - odd)
                    if s == 9:
                        if ps in (1, 2):
                            silu(ps, pq)
                        if ps == 1:
                            split_hi(ps, pq)
                        if ps == 3:
                            ln_std(LN_BEFORE[ps] + pq)
                    if s == 11:
                        if ps == 2:
                            ln_std(LN_BEFORE[ps] + pq)
                        if ps == 3:
                            ln_relu(ps, pq)
                    if s == 12 and ps == 2:
                        ln_relu(ps, pq)

            def prod_out(sweep, q, par):
                g = (sweep - 1) * NG + q
                act.wait_ge(sub_used, (g + 1) * NS)
                act.wait_ge(z_ready, Z0 if sweep == 1 and isinstance(q, int) and q == 0 else Z0 + g - 1)
                act.activation(prod_t[:, par, :], prod_ps[par][:, :], ACT.Copy).then_inc(prod_free, 1)

            def silu(sweep, q):
                act.wait_ge(zt_ready, 2 + ZT_BEFORE[sweep] + q + 1)
                if sweep == 1:
                    act.wait_ge(h_ready, SPLIT_BEFORE[1] + q)
                    act.activation(act_raw[:, :], zt[:, :], ACT.Silu).then_inc(act_ready, 1)
                else:
                    act.activation(zt[:, :], zt[:, :], ACT.Silu).then_inc(silu_ready, 1)

            for sweep in range(1, SWEEPS + 1):
                run_groups(act, sweep, group)
            prod_out(SWEEPS, NG - 1, 1)

        @block.vector
        def _(dve):
            dve.memset(acc[:, :], 0.0).then_inc(acc_clear, 1)

            def prime(s, n):
                dve.sem_inc(s, n)

            for s, n in ((turn_free, 2), (at_free, 4), (nat_free, 4), (row_free, 2), (col_free, 1),
                         (z_free, 2), (zt_ready, 2), (prod_free, 2)):
                prime(s, n)

            def carry_wait():
                dve.memset(carrier[:, :], 0.0)

            def ln_stats(sweep, q):
                n = LN_BEFORE[sweep] + q
                if sweep > 0:
                    carry_wait()
                for b in range(GB):
                    last = dve.bn_stats(stats[:, b, :], x_sb[:, GB * q + b, :])
                last.then_inc(stats_ready, 1)
                dve.wait_ge(stats_ready, n + 1)
                carry_wait()
                for b in range(GB):
                    last = dve.bn_aggr(mv[:, b, :], stats[:, b, :])
                last.then_inc(mv_ready, 1)

            def ln_affine(sweep, q):
                n = LN_BEFORE[sweep] + q
                dve.wait_ge(std_ready, n + 1)
                dve.reciprocal(rstd[:, :], std[:, :]).then_inc(rstd_ready, 1)
                dve.wait_ge(rstd_ready, n + 1)
                if sweep in (2, 3):
                    dve.tensor_tensor(lnscale[:, :], rstd[:, :], d_isqrt[:, ds(GB * q, GB)], ALU.mult)\
                       .then_inc(lnscale_ready, 1)
                else:
                    dve.tensor_copy(lnscale[:, :], rstd[:, :]).then_inc(lnscale_ready, 1)
                dve.wait_ge(lnscale_ready, n + 1)
                dve.scalar_tensor_tensor(out=lnbias[:, :], in0=mv[:, :, 0], scalar=-1.0, in1=lnscale[:, :],
                                         op0=ALU.mult, op1=ALU.mult).then_inc(lnbias_ready, 1)

            dve.wait_ge(x_in[0], 16)
            for q in range(NG):
                if q == NG // 2:
                    dve.wait_ge(x_in[1], 16)
                ln_stats(-1, q)
                ln_affine(-1, q)

            def load_hc(c):
                dve.wait_ge(row_free, 2 + NG * c)
                dve.tensor_copy(hc_hi, h_hi[0][:, ds(CB * c, CB), :].bitcast(F32)).then_inc(hc_ready, 1)
                dve.tensor_copy(hc_lo, h_lo[0][:, ds(CB * c, CB), :].bitcast(F32)).then_inc(hc_ready, 1)

            def turn_out(c, g, k):
                s = (c * NG + g) * CB + k
                half = 2 * g + k // 4
                dve.wait_ge(at_hi_done, s + 1)
                if k % 4 == 0 and g > 0:
                    dve.wait_ge(stored[half % 2], 16 * (c * NG + g))
                dve.tensor_copy(at_raw[:, half % 2, (k % 4) * GW:(k % 4 + 1) * GW], turn_ps[k % 2][:, :])\
                   .then_inc(at_raw_done, 1)
                dve.tensor_tensor(atb(a_lo, k), turn_ps[k % 2][:, :], atb(a_hi, k).bitcast(F32), ALU.subtract)\
                   .then_inc(at_lo_done, 1)

            def row_out(c, g):
                u = c * NG + g
                dve.wait_ge(at_free, 4 + (u + 1) * CB)
                dve.tensor_tensor(acc[:, g * GW:(g + 1) * GW], row_ps[g % 2][:, :], acc[:, g * GW:(g + 1) * GW],
                                  ALU.add).then_inc(row_free, 1)

            def link(ins, n):
                ins.then_inc(deg_step, 1)
                dve.wait_ge(deg_step, n)

            def inverse_degree(dst, part, start):
                link(dve.tensor_reduce(deg[:, 0, :], part, AX_X, ALU.add), start + 1)
                dve.tensor_scalar(deg[:, 1, :], deg[:, 0, :], 0.0, None, ALU.max).then_inc(deg_step, 1)
                link(dve.tensor_scalar(deg[:, 2, :], deg[:, 0, :], 0.0, None, ALU.is_le), start + 3)
                link(dve.tensor_tensor(deg[:, 3, :], deg[:, 1, :], deg[:, 2, :], ALU.add), start + 4)
                link(dve.reciprocal(dst, deg[:, 3, :]), start + 5)

            def add_scaled(zi, bank, block0, inv):
                dve.wait_ge(z_ready, zi + 1)
                for b in range(GB):
                    last = dve.scalar_tensor_tensor(out=x_sb[:, block0 + b, :], in0=z_ps[bank][:, b * D:(b + 1) * D],
                                                    scalar=inv[:, ds(block0 + b, 1)], in1=x_sb[:, block0 + b, :],
                                                    op0=ALU.mult, op1=ALU.add)
                last.then_inc(z_free, 1)

            def chunk_out(c):
                for half in range(2):
                    inverse_degree(inv_col[:, ds(CB * c + GB * half, GB)],
                                   col_part[:, ds(CB * c + GB * half, GB), :], DEG_COL * c + 5 * half)
                for half in range(2):
                    add_scaled(2 * c + half, half, CB * c + GB * half, inv_col)

            def group_out(g):
                dve.wait_ge(nat_hi_done, ((NCH - 1) * NG + g + 1) * GB)
                inverse_degree(inv_row[:, GB * g:GB * g + GB], row_part[:, GB * g:GB * g + GB, :],
                               (NCH - 1) * DEG_COL + g * DEG_ROW)
                dve.wait_ge(z_free, 2 + 2 * (NCH - 1) + g)
                add_scaled(2 * (NCH - 1) + g, g % 2, GB * g, inv_row)

            def sweep0(c, last):
                for g in range(NG):
                    for k in range(CB):
                        turn_out(c, g, k)
                        if g == 0 and k == 0:
                            load_hc(c)
                        if g >= 1 and k == 3:
                            row_out(c, g - 1)
                        if last and g >= 1 and k == 5:
                            group_out(g - 1)
                            if g - 1 < NG - 2:
                                dve.wait_ge(z_free, 2 + 2 * (NCH - 1) + g)
                                ln_stats(0, g - 1)
                        if last and g >= 2 and k == 0:
                            ln_affine(0, g - 2)
                row_out(c, NG - 1)

            dve.wait_ge(acc_clear, 1)
            dve.wait_ge(h_ready, NG)
            dve.wait_ge(const_in, 16 * 8)
            with dve.Fori(0, NCH - 1) as c:
                sweep0(c, False)
                chunk_out(c)
                for half in range(2):
                    dve.wait_ge(stored[half], 16 * NG * (c + 1))
            sweep0(NCH - 1, True)
            group_out(NG - 1)
            for half in range(2):
                inverse_degree(inv_col[:, NB - CB + GB * half:NB - CB + GB * half + GB],
                               col_part[:, NB - CB + GB * half:NB - CB + GB * half + GB, :],
                               (NCH - 1) * DEG_COL + NG * DEG_ROW + 5 * half)
            dve.wait_ge(z_free, 2 + Z0 - 2)
            for half in range(2):
                add_scaled(Z0 - 2 + half, half, NB - CB + GB * half, inv_col)
            dve.wait_ge(z_free, 2 + Z0)
            for q in (NG - 2, NG - 1):
                ln_stats(0, q)
                ln_affine(0, q)
            dve.tensor_reduce(deg_sum[:, :], row_part[:, :, :], AX_X, ALU.add).then_inc(deg_step, 1)
            dve.wait_ge(deg_step, DEG_ALL - 1)
            dve.tensor_scalar(d_isqrt[:, :], deg_sum[:, :], 1.0, None, ALU.add).then_inc(deg_step, 1)
            dve.wait_ge(dsq_ready, 1)
            dve.reciprocal(d_isqrt[:, :], d_isqrt[:, :]).then_inc(dsq_ready, 1)
            dve.wait_ge(dsq_ready, 2)

            def z_out(sweep, q, par):
                g = (sweep - 1) * NG + q
                bias = b_sb[:, B_OF[sweep]:B_OF[sweep] + 1, :].to_broadcast([P, GB, D])
                dve.wait_ge(z_ready, Z0 + g + 1)
                z4 = z_ps[par][:, :].rearrange("p (b f) -> p b f", b=GB)
                zt4 = zt[:, :].rearrange("p (b f) -> p b f", b=GB)
                if sweep in (1, 2):
                    if sweep == 1 and not (isinstance(q, int) and q == 0):
                        dve.wait_ge(act_ready, SPLIT_BEFORE[1] + q)
                    if sweep == 2 and isinstance(q, int) and q == 0:
                        dve.wait_ge(act_ready, SPLIT_BEFORE[1] + NG)
                    dve.tensor_tensor(zt4, z4, bias, ALU.add).then_inc(zt_ready, 1)
                else:
                    for b in range(GB):
                        last = dve.scalar_tensor_tensor(out=zt[:, b * D:(b + 1) * D], in0=z_ps[par][:, b * D:(b + 1) * D],
                                                        scalar=d_isqrt[:, ds(GB * q + b, 1)],
                                                        in1=b_sb[:, B_OF[sweep], :], op0=ALU.mult, op1=ALU.add)
                    last.then_inc(zt_ready, 1)
                    dve.wait_ge(zt_ready, 2 + ZT_BEFORE[sweep] + q + 1)
                    dve.scalar_tensor_tensor(out=x_sb[:, ds(GB * q, GB), :], in0=zt4, scalar=0.0,
                                             in1=x_sb[:, ds(GB * q, GB), :], op0=ALU.max, op1=ALU.add)\
                       .then_inc(x_upd, 1)

            def group(sweep, q, odd):
                ps, pq = before(sweep, q)
                for s in range(NS):
                    sidx = ((sweep - 1) * NG + q) * NS + s
                    dve.wait_ge(sub_hi, sidx + 1)
                    dve.tensor_tensor(sub(a_lo, s), sub_raw(s), sub(a_hi, s).bitcast(F32), ALU.subtract)\
                       .then_inc(sub_lo, 1)
                    if ps == 0:
                        continue
                    if s == 7:
                        z_out(ps, pq, 1 - odd)
                    if ps == 3 and s == 8:
                        dve.wait_ge(x_upd, XUPD_BEFORE[3] + pq + 1)
                        ln_stats(3, pq)
                    if ps == 3 and s == 10:
                        ln_affine(3, pq)
                    if ps == 2 and s == 9:
                        x_plus_silu(pq)
                    if ps == 2 and s == 11:
                        ln_affine(2, pq)

            def x_plus_silu(q):
                dve.wait_ge(silu_ready, q + 1)
                zt4 = zt[:, :].rearrange("p (b f) -> p b f", b=GB)
                dve.tensor_tensor(x_sb[:, ds(GB * q, GB), :], zt4, x_sb[:, ds(GB * q, GB), :], ALU.add)\
                   .then_inc(x_upd, 1)
                dve.wait_ge(x_upd, q + 1)
                ln_stats(2, q)

            for sweep in range(1, SWEEPS + 1):
                run_groups(dve, sweep, group)
            z_out(SWEEPS, NG - 1, 1)

        @block.tensor
        def _(pe):
            pe.wait_ge(ident_made, 3)

            def split_products(ps, hi_w, lo_w, hi_a, lo_a, start, stop):
                pe.matmul(ps, hi_w, hi_a, start=start, stop=False)
                pe.matmul(ps, lo_w, hi_a, start=False, stop=False)
                return pe.matmul(ps, hi_w, lo_a, start=False, stop=stop)

            def weight_product(bank, src, w, zi, sweep0_z=True):
                if sweep0_z:
                    pe.wait_ge(z_free, zi + 1)
                else:
                    pe.wait_ge(zt_ready, zi + 1)
                for b in range(GB):
                    last = pe.matmul(z_ps[bank][:, b * D:(b + 1) * D], src[:, b * P:(b + 1) * P], w_sb[:, w, :],
                                     start=True, stop=True)
                last.then_inc(z_ready, 1)

            def turn(c, g, k):
                s = (c * NG + g) * CB + k
                if k == 0:
                    for a in range(GB):
                        pe.wait_ge(nat_in[4 * (g % 2) + a], 16 * (c * (NG // 2) + g // 2) + 16)
                if k >= 2 or g > 0:
                    pe.wait_ge(at_lo_done, s - 1)
                for a in range(GB):
                    last = pe.transpose(turn_ps[k % 2][:, a * P:(a + 1) * P], nat_raw(g, a)[:, k * P:(k + 1) * P],
                                        ident[:, :])
                last.then_inc(turned, 1)

            def col_product(c, g, k):
                a, half = k // 2, k % 2
                n = (c * NG + g) * GB + a
                if g == 0 and k == 0:
                    pe.wait_ge(col_free, c + 1)
                if half == 0:
                    pe.wait_ge(nat_lo_done, n + 1)
                cols = slice(half * GW, (half + 1) * GW)
                last = split_products(col_ps[half][:, :], h_hi[0][:, GB * g + a, :], h_lo[0][:, GB * g + a, :],
                                      nat(a_hi, a)[:, cols], nat(a_lo, a)[:, cols],
                                      g == 0 and a == 0, g == NG - 1 and a == GB - 1)
                if half == 1:
                    last.then_inc(nat_free, 1)

            def row_product(c, g, k):
                s = (c * NG + g) * CB + k
                if k == 0:
                    pe.wait_ge(row_free, c * NG + g + 1)
                if g == 0 and k == 0:
                    pe.wait_ge(hc_ready, 2 * c + 2)
                pe.wait_ge(at_lo_done, s + 1)
                last = split_products(row_ps[g % 2][:, :], hc_hi[:, k, :], hc_lo[:, k, :],
                                      atb(a_hi, k), atb(a_lo, k), k == 0, k == CB - 1)
                last.then_inc(at_free, 1)

            def sweep0(c, last):
                for g in range(NG):
                    for k in range(CB):
                        turn(c, g, k)
                        col_product(c, g, k)
                        if k >= 1:
                            row_product(c, g, k - 1)
                        elif g >= 1:
                            row_product(c, g - 1, CB - 1)
                        if last and g >= 1 and k == 4:
                            pe.wait_ge(row_free, 2 + c * NG + g)
                            weight_product((g - 1) % 2, acc[:, (g - 1) * GW:g * GW], 0, 2 * (NCH - 1) + g - 1)
                row_product(c, NG - 1, CB - 1)

            pe.wait_ge(h_ready, NG)
            pe.wait_ge(const_in, 16 * 8)
            with pe.Fori(0, NCH - 1) as c:
                sweep0(c, False)
                pe.wait_ge(col_free, c + 2)
                for half in range(2):
                    weight_product(half, prod_t[:, half, :], 1, 2 * c + half)
            sweep0(NCH - 1, True)
            pe.wait_ge(row_free, 2 + UNITS)
            weight_product(1, acc[:, N - GW:N], 0, Z0 - 3)
            pe.wait_ge(col_free, NCH + 1)
            for half in range(2):
                weight_product(half, prod_t[:, half, :], 1, Z0 - 2 + half)

            def group(sweep, q, odd):
                s_in = SET_OF[sweep - 1]
                hi, lo = h_hi[s_in], h_lo[s_in]
                ps, pq = before(sweep, q)
                gidx = (sweep - 1) * NG + q
                bank = prod_ps[odd][:, :]
                first_group = isinstance(q, int) and q == 0
                if sweep == 1 and first_group:
                    pe.wait_ge(at_lo_done, STEPS)
                pe.wait_ge(prod_free, gidx + 1)
                for s in range(NS):
                    sidx = gidx * NS + s
                    if first_group and s % 2 == 0:
                        pe.wait_ge(h_ready, SPLIT_BEFORE[sweep - 1] + s // 2 + 1)
                    pe.wait_ge(sub_hi, sidx + 1)
                    for b in range(SB2):
                        cols = slice(b * GW, (b + 1) * GW)
                        pe.matmul(bank, hi[:, SB2 * s + b, :], sub(a_hi, s)[:, cols], start=(s == 0 and b == 0), stop=False)
                        pe.matmul(bank, lo[:, SB2 * s + b, :], sub(a_hi, s)[:, cols], start=False, stop=False)
                    pe.wait_ge(sub_lo, sidx + 1)
                    for b in range(SB2):
                        cols = slice(b * GW, (b + 1) * GW)
                        last = pe.matmul(bank, hi[:, SB2 * s + b, :], sub(a_lo, s)[:, cols], start=False,
                                         stop=(s == NS - 1 and b == SB2 - 1))
                    last.then_inc(sub_used, 1)
                    if s == NS - 3 and sweep >= 3:
                        identity_product(sweep, q, bank)
                    if s == 4 and sweep == 1 and first_group:
                        pe.wait_ge(z_free, 2 + Z0)
                    if s == 4 and ps > 0:
                        finish(ps, pq, 1 - odd)

            def identity_product(sweep, q, bank):
                pe.wait_ge(hd_ready, 2 * ((sweep - 3) * NG + q) + 2)
                for b in range(GB):
                    for part in (hd_hi, hd_lo):
                        pe.matmul(bank[:, b * P:(b + 1) * P], part[:, b, :], ident_r[:, :], start=False, stop=False,
                                  skip_group_check=True)

            def finish(sweep, q, par):
                g = (sweep - 1) * NG + q
                pe.wait_ge(prod_free, 2 + g + 1)
                weight_product(par, prod_t[:, par, :], W_OF[sweep], g, False)

            for sweep in range(1, SWEEPS + 1):
                run_groups(pe, sweep, group)
            finish(SWEEPS, NG - 1, 1)


_INS = ['x', 'adj', 'L0_gnn_W_in', 'L0_gnn_W_out', 'L1_gnn_W', 'L1_gnn_b', 'L2_gnn_W', 'L2_gnn_b',
        'L3_gnn_W', 'L3_gnn_b']
_OUTS = [((4096, 128), 'float32')]


def kernel(**inputs):
    import numpy as _np
    import concourse.bacc as _bacc
    from concourse import mybir as _mybir
    from concourse.bass_utils import run_bass_kernel_spmd as _run

    nc = _bacc.Bacc("TRN2", target_bir_lowering=False, num_devices=1)
    arrays, args = {}, []
    for name in _INS:
        a = _np.ascontiguousarray(inputs[name])
        arrays[f"in_{name}_dram"] = a
        args.append(nc.dram_tensor(f"in_{name}_dram", a.shape, _mybir.dt.from_np(a.dtype), kind="ExternalInput").ap())
    for i, (shape, dtype) in enumerate(_OUTS):
        dt = _mybir.dt.from_np(_np.dtype(dtype))
        args.append(nc.dram_tensor(f"out_{i}_dram", shape, dt, kind="ExternalOutput").ap())
    build_gnn_stack(nc, *args)
    r = _run(nc, [arrays], core_ids=[0])
    got = tuple(r.results[0][f"out_{i}_dram"] for i in range(len(_OUTS)))
    return got[0]
```

```python
from contextlib import ExitStack

import concourse.bass as bass
from concourse import mybir

F32 = mybir.dt.float32
F32R = mybir.dt.float32r
ALU = mybir.AluOpType
ACT = mybir.ActivationFunctionType
AX_X = mybir.AxisListType.X
ds = bass.ds

P = 128
EPS = 1e-5


def build_gnn_stack(nc, x, adj, w_in, w_out, w1, b1, w2, b2, w3, b3, out):
    N, D = x.shape
    assert D == P and N % 1024 == 0
    NB = N // P
    GB = 4
    GW = GB * P
    NG = N // GW
    CB = 8
    CW = CB * P
    NCH = N // CW
    UNITS = NCH * NG
    STEPS = UNITS * CB
    SUBS = UNITS * GB
    SB2 = 2
    NS = NB // SB2
    NT = NS // 2
    SWEEPS = 4
    Z0 = 2 * NG
    Z_ROW = 2 * (NCH - 1)
    FIRST_STATS, FIRST_STD, FIRST_AFFINE = [(0, 2), (1, 5), (3, 5)], [(0, 6), (1, 7), (3, 7)], [(0, 7), (2, 1), (4, 1)]
    POOL_LO = (2, 8)
    ACT_RAW = (3, 7)

    adj_t = nc.dram_tensor("adj_t_scratch", (NG, P, NB * GW), F32, kind="Internal").ap()

    ctx = ExitStack()
    with ctx:
        def sb(name, shape, dt=F32):
            return ctx.enter_context(nc.sbuf_tensor(name, shape, dt))

        def sem(name):
            return ctx.enter_context(nc.semaphore(name))

        x_sb = sb("x_sb", [P, NB, D])
        h_hi = [sb(f"h_hi{i}", [P, NB, D], F32R) for i in range(2)]
        h_lo = [sb(f"h_lo{i}", [P, NB, D], F32R) for i in range(2)]
        raw = sb("raw", [P, 8, 1024])
        a_hi = sb("a_hi", [P, 6, 1024], F32R)
        a_lo = sb("a_lo", [P, 6, 1024], F32R)
        at_raw = sb("at_raw", [P, 2, GB * GW])
        acc = sb("acc", [P, N])
        prod_t = sb("prod_t", [P, 2, GW])
        w_sb = sb("w_sb", [P, 5, D])
        b_sb = sb("b_sb", [P, 3, D])
        ident = sb("ident", [P, P])
        ident_r = sb("ident_r", [P, P], F32R)
        row_part = sb("row_part", [P, NB, NCH])
        col_part = sb("col_part", [P, NB, NG])
        deg = sb("deg", [P, 4, GB])
        deg_sum = sb("deg_sum", [P, NB])
        inv_row = sb("inv_row", [P, NB])
        inv_col = sb("inv_col", [P, NB])
        d_isqrt = sb("d_isqrt", [P, NB])
        zt = sb("zt", [P, GW])
        act_raw = sb("act_raw", [P, GW])
        stats = sb("stats", [P, GB, 6])
        mv = sb("mv", [P, GB, 2])
        std = sb("std", [P, GB])
        rstd = sb("rstd", [P, GB])
        lnscale = sb("lnscale", [P, GB])
        lnbias = sb("lnbias", [P, GB])
        carrier = sb("carrier", [P, 1])
        eps_sb = sb("eps_sb", [P, 1])
        one_sb = sb("one_sb", [P, 1])
        minus_half = sb("minus_half", [P, 1])
        newton = sb("newton", [P, 3, GB])

        banks = [ctx.enter_context(nc.psum_tensor(f"bank{i}", [P, 512], F32)) for i in range(8)]
        turn_ps = banks[0:2] + banks[6:8]
        row_ps, col_ps = banks[2:4], banks[4:6]
        z_ps = banks[6:8]
        prod_ps = banks[0:2]

        hc_hi, hc_lo = h_hi[1][:, NB - CB:NB, :], h_lo[1][:, NB - CB:NB, :]
        hd_hi = a_hi[:, 4, 0:GW].rearrange("p (b f) -> p b f", b=GB)
        hd_lo = a_lo[:, 4, 0:GW].rearrange("p (b f) -> p b f", b=GB)

        XP = NB // 4
        stats0 = zt[:, 0:6 * NB].rearrange("p (b s) -> p b s", s=6)
        mv0 = zt[:, 256:256 + 2 * NB].rearrange("p (b s) -> p b s", s=2)
        std0, rstd0, bias0 = (zt[:, 384 + i * NB:384 + (i + 1) * NB] for i in range(3))

        def at_raw_block(k):
            return at_raw[:, k // 4, (k % 4) * GW:(k % 4 + 1) * GW]

        def nat_raw(u, a):
            return raw[:, 4 * (u % 2) + a, :]

        def nat(t, a):
            return t[:, a, :]

        def atb(t, k):
            k = k % 4
            return t[:, 4 + k // 2, (k % 2) * GW:(k % 2 + 1) * GW]

        def sub_raw(sweep, q, s):
            if kept(q, s // 2):
                return kept_tile(q, s // 2)[:, (s % 2) * 1024:(s % 2 + 1) * 1024]
            return raw[:, 2 * load_number(sweep, q, s // 2)[1] + s % 2, :]

        def sub(t, s):
            return t[:, s % 4, :]

        x_in = [sem(f"x_in{i}") for i in range(4)]
        stats0_ready = sem("stats0_ready")
        mv0_ready = sem("mv0_ready")
        std0_ready = sem("std0_ready")
        rstd0_ready = sem("rstd0_ready")
        bias0_ready = sem("bias0_ready")
        const_in = sem("const_in")
        ident_made = sem("ident_made")
        ones_made = sem("ones_made")
        nat_in = [sem(f"nat_in{i}") for i in range(8)]
        tile_in = [sem(f"tile_in{i}") for i in range(4)]
        stored = [sem(f"stored{i}") for i in range(4)]
        kept_in = [sem(f"kept_in{i}") for i in range(2)]
        turned = sem("turned")
        at_hi_done = sem("at_hi_done")
        at_lo_done = sem("at_lo_done")
        at_free = sem("at_free")
        nat_hi_done = sem("nat_hi_done")
        nat_lo_done = sem("nat_lo_done")
        nat_free = sem("nat_free")
        row_free = sem("row_free")
        col_free = sem("col_free")
        hc_ready = sem("hc_ready")
        acc_clear = sem("acc_clear")
        z_ready = sem("z_ready")
        z_free = sem("z_free")
        sub_hi = sem("sub_hi")
        sub_lo = sem("sub_lo")
        sub_lo_pool = sem("sub_lo_pool")
        sub_used = sem("sub_used")
        prod_free = sem("prod_free")
        hd_ready = sem("hd_ready")
        zt_ready = sem("zt_ready")
        silu_ready = sem("silu_ready")
        x_upd = sem("x_upd")
        stats_ready = sem("stats_ready")
        mv_ready = sem("mv_ready")
        std_ready = sem("std_ready")
        rstd_ready = sem("rstd_ready")
        lnscale_ready = sem("lnscale_ready")
        lnbias_ready = sem("lnbias_ready")
        newton_done = sem("newton_done")
        normed = sem("normed")
        act_ready = sem("act_ready")
        h_hi_ready = sem("h_hi_ready")
        h_ready = sem("h_ready")
        deg_step = sem("deg_step")
        dsq_ready = sem("dsq_ready")
        out_done = sem("out_done")

        LN_BEFORE = {0: 0, 2: NG, 3: 2 * NG}
        SPLIT_BEFORE = {-1: 0, 0: NG, 1: 2 * NG, 2: 3 * NG, 3: 4 * NG}
        XUPD_BEFORE = {2: 0, 3: NG, 4: 2 * NG}
        ZT_BEFORE = {1: 0, 2: NG, 3: 2 * NG, 4: 3 * NG}
        SET_OF = {-1: 0, 0: 1, 1: 0, 2: 1, 3: 0}
        W_OF = {1: 2, 2: 2, 3: 3, 4: 4}
        B_OF = {1: 0, 2: 0, 3: 1, 4: 2}

        DEG_COL = 5 * 2
        DEG_ROW = 5
        DEG_ALL = NCH * DEG_COL + NG * DEG_ROW + 2

        def run_groups(eng, sweep, group):
            group(sweep, 0, 0)
            with eng.Fori(0, (NG - 2) // 2) as m:
                group(sweep, 2 * m + 1, 1)
                group(sweep, 2 * m + 2, 0)
            group(sweep, NG - 1, 1)

        TW = 2048
        KEPT = {0: (NT - 2, NT - 1), NG - 1: (NT - 2, NT - 1)}
        LOADS = NG * NT - 4

        def kept(q, t):
            return isinstance(q, int) and t in KEPT.get(q, ())

        def kept_tile(q, t):
            i = t - KEPT[q][0]
            return acc[:, i * TW:(i + 1) * TW] if q == 0 else at_raw[:, i, :]

        def load_number(sweep, q, t):
            skipped = 0 if isinstance(q, int) and q == 0 else len(KEPT[0])
            t = t - skipped
            return (sweep - 1) * (LOADS // 4) + q * (NT // 4) + t // 4, t % 4

        def tile_before(sweep, q, t, n):
            base = (sweep - 1) * NG * NT
            if isinstance(q, int):
                at = q * NT + t
                while n:
                    at -= 1
                    if not kept(at % (NG * NT) // NT, at % NT):
                        n -= 1
                return base + at
            return base + q * NT + t - n

        AT_PROD, AT_WEIGHTS, AT_Z, AT_SILU = 3, 3, 7, 8
        AT_STATS = {1: None, 2: 9, 3: 8, 4: None}
        AT_STD = 10
        AT_AFFINE = {1: None, 2: 12, 3: 11, 4: None}
        AT_HI = {1: 9, 2: 14, 3: 14, 4: None}
        POOL_INC = NS // len(POOL_LO)

        def pool_lo_count(sweep, q, t):
            if isinstance(q, int):
                tile = tile_before(sweep, q, t, 4)
                group, tile = tile // NT, tile % NT
            else:
                group, tile = (sweep - 1) * NG + q + (t - 4) // NT, (t - 4) % NT
            return group * NS + POOL_INC * (POOL_LO.index(2 * tile) + 1) if 2 * tile in POOL_LO else None

        def normed_by_vector(sweep, q):
            return sweep in (2, 3) or sweep == 0 and q >= NG - 2

        def before(sweep, q):
            if isinstance(q, int) and q == 0:
                return sweep - 1, NG - 1
            return sweep, q - 1

        block = ctx.enter_context(nc.Block())

        @block.sync
        def _(sp):
            xv = x.rearrange("(b p) d -> p b d", p=P)

            def load_x(i):
                sp.dma_start(x_sb[:, i * XP:(i + 1) * XP, :], xv[:, i * XP:(i + 1) * XP, :]).then_inc(x_in[i], 16)

            def load_nat(c, g):
                for a in range(GB):
                    sp.dma_start(nat_raw(g, a), adj[(GB * g + a) * P:(GB * g + a + 1) * P, ds(c * CW, CW)])\
                      .then_inc(nat_in[4 * (g % 2) + a], 16)

            load_x(0)
            load_nat(0, 0)
            load_x(1)
            load_nat(0, 1)
            for i in (2, 3):
                load_x(i)
            for i, w in enumerate((w_in, w_out, w1, w2, w3)):
                sp.dma_start(w_sb[:, i, :], w).then_inc(const_in, 16)
            for i, b in enumerate((b1, b2, b3)):
                sp.dma_start(b_sb[:, i, :], b.rearrange("(a n) -> a n", a=1).to_broadcast([P, D])).then_inc(const_in, 16)

            def store(c, g, j):
                sp.wait_ge(at_lo_done, c * NG * CB + g * CB + 2 * j + 2)
                sp.dma_start(adj_t[g, :, ds(c * CB * GW + 2 * j * GW, 2 * GW)],
                             at_raw[:, j // 2, (j % 2) * 2 * GW:(j % 2 + 1) * 2 * GW]).then_inc(stored[j], 16)

            def sweep0(c, last):
                for g in range(NG):
                    if last and g == NG - 1:
                        break
                    for j in range(3):
                        store(c, g, j)
                    if not (last and g == NG - 2):
                        sp.wait_ge(turned, (c * NG + g) * CB + CB)
                        sp.wait_ge(nat_lo_done, (c * NG + g) * GB + GB)
                        load_nat(c + (g + 2) // NG, (g + 2) % NG)
                    store(c, g, 3)

            with sp.Fori(0, NCH - 1) as c:
                sweep0(c, False)
            sweep0(NCH - 1, True)

            for j in range(4):
                sp.wait_ge(stored[j], 16 * ((NCH - 1) * NG + 1))

            def load_tiles(sweep, q):
                for t in range(NT):
                    if sweep == 1 and isinstance(q, int) and q == 0 and t in (0, 2):
                        sp.wait_ge(turned, STEPS - (CB if t == 0 else 0))
                        sp.wait_ge(nat_lo_done, SUBS - (GB if t == 0 else 0))
                    if not kept(q, t):
                        n, slot = load_number(sweep, q, t)
                        if not (sweep == 1 and isinstance(q, int) and q == 0 and t < 4):
                            sp.wait_ge(sub_lo, tile_before(sweep, q, t, 4) * 2 + 2)
                            by_pool = pool_lo_count(sweep, q, t)
                            if by_pool is not None:
                                sp.wait_ge(sub_lo_pool, by_pool)
                        sp.dma_start(raw[:, 2 * slot:2 * slot + 2, :].rearrange("p a n -> p (a n)"),
                                     adj_t[q, :, t * TW:(t + 1) * TW]).then_inc(tile_in[slot], 16)
                    elif sweep == 1 and q == 0:
                        if t == KEPT[0][0]:
                            sp.wait_ge(z_ready, Z0 - 2)
                        sp.dma_start(kept_tile(q, t), adj_t[q, :, t * TW:(t + 1) * TW]).then_inc(kept_in[t - KEPT[0][0]], 16)

            for sweep in range(1, SWEEPS + 1):
                load_tiles(sweep, 0)
                if sweep == 1:
                    for j in range(4):
                        sp.wait_ge(stored[j], 16 * (UNITS - 1))
                load_tiles(sweep, 1)
                with sp.Fori(2, NG - 1) as q:
                    load_tiles(sweep, q)
                load_tiles(sweep, NG - 1)

            with sp.Fori(0, NG) as q:
                sp.wait_ge(x_upd, XUPD_BEFORE[4] + q + 1)
                sp.dma_start(out.rearrange("(g b p) d -> g p b d", p=P, b=GB)[q], x_sb[:, ds(GB * q, GB), :])\
                  .then_inc(out_done, 16)
            sp.wait_ge(out_done, 16 * NG)

        @block.gpsimd
        def _(pool):
            pool.memset(ident[:, :], 0.0).then_inc(ident_made, 1)
            pool.memset(eps_sb[:, :], EPS).then_inc(ones_made, 1)
            pool.memset(minus_half[:, :], -0.5)
            pool.memset(one_sb[:, :], 1.0).then_inc(ones_made, 1)
            pool.wait_ge(ident_made, 1)
            pool.affine_select(out=ident[:, :], in_=ident[:, :], compare_op=ALU.not_equal, fill=1.0,
                               base=0, pattern=[[-1, P]], channel_multiplier=1).then_inc(ident_made, 1)

            def split_lo(sweep, q):
                s = SET_OF[sweep]
                pool.wait_ge(h_hi_ready, SPLIT_BEFORE[sweep] + q + 1)
                pool.tensor_tensor(h_lo[s][:, ds(GB * q, GB), :],
                                   act_raw[:, :].rearrange("p (b f) -> p b f", b=GB),
                                   h_hi[s][:, ds(GB * q, GB), :].bitcast(F32), ALU.subtract).then_inc(h_ready, 1)

            def nat_split(c, g, a):
                n = (c * NG + g) * GB + a
                pool.wait_ge(nat_hi_done, n + 1)
                pool.tensor_tensor(nat(a_lo, a), nat_raw(g, a), nat(a_hi, a).bitcast(F32),
                                   ALU.subtract).then_inc(nat_lo_done, 1)

            def load_hc(c, j):
                pool.wait_ge(at_free, 4 + c * NG * CB - CB + 2 * j + 2)
                for dst, src in ((hc_hi, h_hi[0]), (hc_lo, h_lo[0])):
                    pool.tensor_copy(dst[:, 2 * j:2 * j + 2, :], src[:, ds(CB * c + 2 * j, 2), :].bitcast(F32))\
                        .then_inc(hc_ready, 1)

            def sweep0(c, first, last):
                for g in range(NG):
                    for a in range(GB):
                        if last and a == 1 and g >= 3:
                            split_lo(0, g - 3)
                        nat_split(c, g, a)
                        if not first and g == 0 and a < 2:
                            load_hc(c, 2 + a)
                        if first and a == 2 and g < NG - 1:
                            split_lo(-1, g + 1)
                        if not last and g == NG - 1 and a >= 2:
                            load_hc(c + 1, a - 2)

            split_lo(-1, 0)
            sweep0(0, True, False)
            with pool.Fori(1, NCH - 1) as c:
                sweep0(c, False, False)
            sweep0(NCH - 1, False, True)
            split_lo(0, NG - 3)

            def pool_rstd(n):
                pool.wait_ge(mv_ready, n + 1)
                pool.tensor_tensor(std[:, :], mv[:, :, 1], eps_sb[:, :].to_broadcast([P, GB]), ALU.add)\
                    .then_inc(std_ready, 1)
                pool.wait_ge(std_ready, n + 1)
                pool.tensor_tensor(rstd[:, :], std[:, :], minus_half[:, :].to_broadcast([P, GB]), ALU.pow)\
                    .then_inc(rstd_ready, 1)

            def sub_split(sweep, q, s):
                g = (sweep - 1) * NG + q
                pool.wait_ge(sub_hi, g * NS + s + 1)
                pool.tensor_tensor(sub(a_lo, s), sub_raw(sweep, q, s), sub(a_hi, s).bitcast(F32), ALU.subtract)\
                    .then_inc(sub_lo_pool, POOL_INC)

            def group(sweep, q, odd):
                sub_split(sweep, q, POOL_LO[0])
                if sweep >= 3:
                    if not (sweep == 3 and isinstance(q, int) and q == 0):
                        pool.wait_ge(sub_used, ((sweep - 1) * NG + q) * NS)
                    s = SET_OF[sweep - 1]
                    pool.wait_ge(h_ready, SPLIT_BEFORE[sweep - 1] + q + 1)
                    pool.tensor_copy(hd_hi, h_hi[s][:, ds(GB * q, GB), :].bitcast(F32)).then_inc(hd_ready, 1)
                    pool.tensor_copy(hd_lo, h_lo[s][:, ds(GB * q, GB), :].bitcast(F32)).then_inc(hd_ready, 1)
                for s in POOL_LO[1:]:
                    sub_split(sweep, q, s)
                ps, pq = before(sweep, q)
                if ps == 2:
                    pool_rstd(LN_BEFORE[2] + pq)
                for p in ((NG - 2, NG - 1) if ps == 0 else (pq,)):
                    if ps <= 3:
                        split_lo(ps, p)

            for sweep in range(1, SWEEPS + 1):
                run_groups(pool, sweep, group)

        @block.scalar
        def _(act):
            act.wait_ge(ident_made, 2)
            act.activation(ident_r[:, :], ident[:, :], ACT.Copy).then_inc(ident_made, 1)
            act.wait_ge(ones_made, 2)

            def first_std(i):
                act.wait_ge(mv0_ready, i + 1)
                act.activation(std0[:, i * XP:(i + 1) * XP], mv0[:, i * XP:(i + 1) * XP, 1], ACT.Sqrt,
                               bias=eps_sb[:, 0:1]).then_inc(std0_ready, 1)

            def ln_std(n):
                act.wait_ge(mv_ready, n + 1)
                act.activation(std[:, :], mv[:, :, 1], ACT.Sqrt, bias=eps_sb[:, 0:1]).then_inc(std_ready, 1)

            def split_hi(sweep, q):
                m = SPLIT_BEFORE[sweep] + q
                if normed_by_vector(sweep, q):
                    act.wait_ge(normed, LN_BEFORE[sweep] + q - (NG - 2) + 1)
                    act.activation(act_raw[:, :], act_raw[:, :], ACT.Relu).then_inc(act_ready, 1)
                act.wait_ge(act_ready, m + 1)
                act.activation(h_hi[SET_OF[sweep]][:, ds(GB * q, GB), :],
                               act_raw[:, :].rearrange("p (b f) -> p b f", b=GB),
                               ACT.Copy).then_inc(h_hi_ready, 1)

            def ln_relu(sweep, q):
                n, m = LN_BEFORE[sweep] + q, SPLIT_BEFORE[sweep] + q
                act.wait_ge(lnbias_ready, n + 1)
                act.wait_ge(h_ready, m)
                for b in range(GB):
                    last = act.activation(act_raw[:, b * D:(b + 1) * D], x_sb[:, GB * q + b, :], ACT.Relu,
                                          bias=lnbias[:, b:b + 1], scale=lnscale[:, b:b + 1])
                last.then_inc(act_ready, 1)
                split_hi(sweep, q)

            def first_relu(q):
                act.wait_ge(bias0_ready, GB * q // XP + 1)
                if q > 0:
                    act.wait_ge(h_ready, q)
                for b in range(GB):
                    n = GB * q + b
                    last = act.activation(act_raw[:, b * D:(b + 1) * D], x_sb[:, n, :], ACT.Relu,
                                          bias=bias0[:, n:n + 1], scale=rstd0[:, n:n + 1])
                last.then_inc(act_ready, 1)
                split_hi(-1, q)

            def nat_hi(c, g, a):
                n = (c * NG + g) * GB + a
                act.wait_ge(nat_in[4 * (g % 2) + a], 16 * (c * (NG // 2) + g // 2) + 16)
                act.wait_ge(nat_free, n + 1)
                act.activation(nat(a_hi, a), nat_raw(g, a), ACT.Copy,
                               accum_out=row_part[:, GB * g + a, ds(c, 1)]).then_inc(nat_hi_done, 1)

            def at_hi(c, g, k):
                s = (c * NG + g) * CB + k
                act.wait_ge(turned, s + 1)
                if k in ACT_RAW:
                    if not (isinstance(c, int) and c == 0 and g == 0):
                        act.wait_ge(stored[k // 2], 16 * (c * NG + g))
                    act.activation(at_raw_block(k), turn_ps[k % 4][:, :], ACT.Copy)
                act.wait_ge(at_free, s + 1)
                act.activation(atb(a_hi, k), turn_ps[k % 4][:, :], ACT.Copy,
                               accum_out=col_part[:, ds(CB * c + k, 1), g]).then_inc(at_hi_done, 1)

            def col_out(c):
                act.wait_ge(nat_free, 4 + (c + 1) * NG * GB)
                for half in range(2):
                    last = act.activation(prod_t[:, half, :], col_ps[half][:, :], ACT.Copy)
                last.then_inc(col_free, 1)

            def sweep0(c, first, last):
                for g in range(NG):
                    for k in range(CB):
                        at_hi(c, g, k)
                        if not first and g == 0 and k == 2:
                            col_out(c - 1)
                        if k % 2 == 0:
                            a = (k // 2 + 1) % GB
                            if a > 0:
                                nat_hi(c, g, a)
                            elif not (last and g == NG - 1):
                                nat_hi(c + (g + 1) // NG, (g + 1) % NG, 0)
                        if first and (g, k) in FIRST_STD:
                            first_std(FIRST_STD.index((g, k)) + 1)
                        if first and g < NG - 1 and k == 3:
                            first_relu(g + 1)
                        if last and g >= 2 and k == 3:
                            ln_std(LN_BEFORE[0] + g - 2)
                        if last and g >= 2 and k == 7:
                            ln_relu(0, g - 2)

            first_std(0)
            first_relu(0)
            nat_hi(0, 0, 0)
            sweep0(0, True, False)
            with act.Fori(1, NCH - 1) as c:
                sweep0(c, False, False)
            sweep0(NCH - 1, False, True)

            def finish_sweep0(s):
                if s == 0:
                    col_out(NCH - 1)
                for i, q in enumerate((NG - 2, NG - 1)):
                    if s == 9 + 2 * i:
                        ln_std(LN_BEFORE[0] + q)
                    if s == 12 + 2 * i:
                        split_hi(0, q)
                if s == 15:
                    act.wait_ge(deg_step, DEG_ALL)
                    act.activation(d_isqrt[:, :], d_isqrt[:, :], ACT.Sqrt).then_inc(dsq_ready, 1)

            def group(sweep, q, odd):
                ps, pq = before(sweep, q)
                for s in range(NS):
                    sidx = ((sweep - 1) * NG + q) * NS + s
                    if s % 2 == 0 and not kept(q, s // 2):
                        turns, slot = load_number(sweep, q, s // 2)
                        act.wait_ge(tile_in[slot], 16 * turns + 16)
                    elif s % 2 == 0 and sweep == 1 and q == 0:
                        act.wait_ge(kept_in[s // 2 - KEPT[0][0]], 16)
                    if sweep == 1 and isinstance(q, int) and q == 0 and s < 4:
                        act.wait_ge(nat_free, SUBS + s + 1)
                    else:
                        act.wait_ge(sub_used, sidx - 3)
                    act.activation(sub(a_hi, s), sub_raw(sweep, q, s), ACT.Copy).then_inc(sub_hi, 1)
                    if ps == 0:
                        finish_sweep0(s)
                        continue
                    if s == AT_PROD:
                        prod_out(ps, pq, 1 - odd)
                    if s == AT_SILU and ps in (1, 2):
                        silu(ps, pq)
                    if s == AT_STD and ps == 3:
                        ln_std(LN_BEFORE[ps] + pq)
                    if s == AT_HI[ps]:
                        split_hi(ps, pq)

            def prod_out(sweep, q, par):
                g = (sweep - 1) * NG + q
                act.wait_ge(sub_used, (g + 1) * NS)
                act.wait_ge(z_ready, Z0 if sweep == 1 and isinstance(q, int) and q == 0 else Z0 + g - 1)
                act.activation(prod_t[:, par, :], prod_ps[par][:, :], ACT.Copy).then_inc(prod_free, 1)

            def silu(sweep, q):
                act.wait_ge(zt_ready, 2 + ZT_BEFORE[sweep] + q + 1)
                if sweep == 1:
                    act.wait_ge(h_ready, SPLIT_BEFORE[1] + q)
                    act.activation(act_raw[:, :], zt[:, :], ACT.Silu).then_inc(act_ready, 1)
                else:
                    act.activation(zt[:, :], zt[:, :], ACT.Silu).then_inc(silu_ready, 1)

            for sweep in range(1, SWEEPS + 1):
                run_groups(act, sweep, group)
            prod_out(SWEEPS, NG - 1, 1)

        @block.vector
        def _(dve):
            dve.memset(acc[:, :], 0.0).then_inc(acc_clear, 1)

            def prime(s, n):
                dve.sem_inc(s, n)

            for s, n in ((at_free, 4), (nat_free, 4), (row_free, 2), (col_free, 1), (zt_ready, 2), (prod_free, 2)):
                prime(s, n)

            def carry_wait():
                dve.memset(carrier[:, :], 0.0)

            def ln_stats(sweep, q):
                n = LN_BEFORE[sweep] + q
                carry_wait()
                for b in range(GB):
                    last = dve.bn_stats(stats[:, b, :], x_sb[:, GB * q + b, :])
                last.then_inc(stats_ready, 1)
                dve.wait_ge(stats_ready, n + 1)
                carry_wait()
                for b in range(GB):
                    last = dve.bn_aggr(mv[:, b, :], stats[:, b, :])
                last.then_inc(mv_ready, 1)

            def ln_affine(sweep, q):
                n = LN_BEFORE[sweep] + q
                if sweep != 2:
                    dve.wait_ge(std_ready, n + 1)
                    dve.reciprocal(rstd[:, :], std[:, :]).then_inc(rstd_ready, 1)
                dve.wait_ge(rstd_ready, n + 1)
                if sweep == 2:
                    dve.tensor_tensor(newton[:, 0, :], rstd[:, :], rstd[:, :], ALU.mult).then_inc(newton_done, 1)
                    dve.tensor_tensor(newton[:, 1, :], rstd[:, :], d_isqrt[:, ds(GB * q, GB)], ALU.mult)\
                       .then_inc(newton_done, 1)
                    dve.wait_ge(newton_done, 3 * q + 1)
                    dve.scalar_tensor_tensor(out=newton[:, 2, :], in0=newton[:, 0, :], scalar=-0.5, in1=std[:, :],
                                             op0=ALU.mult, op1=ALU.mult).then_inc(newton_done, 1)
                    dve.wait_ge(newton_done, 3 * q + 3)
                    dve.scalar_tensor_tensor(out=lnscale[:, :], in0=newton[:, 2, :], scalar=1.5, in1=newton[:, 1, :],
                                             op0=ALU.add, op1=ALU.mult).then_inc(lnscale_ready, 1)
                elif sweep == 3:
                    dve.tensor_tensor(lnscale[:, :], rstd[:, :], d_isqrt[:, ds(GB * q, GB)], ALU.mult)\
                       .then_inc(lnscale_ready, 1)
                else:
                    dve.tensor_copy(lnscale[:, :], rstd[:, :]).then_inc(lnscale_ready, 1)
                dve.wait_ge(lnscale_ready, n + 1)
                dve.scalar_tensor_tensor(out=lnbias[:, :], in0=mv[:, :, 0], scalar=-1.0, in1=lnscale[:, :],
                                         op0=ALU.mult, op1=ALU.mult).then_inc(lnbias_ready, 1)
                if normed_by_vector(sweep, q):
                    dve.wait_ge(lnbias_ready, n + 1)
                    dve.wait_ge(h_ready, SPLIT_BEFORE[sweep] + q)
                    for b in range(GB):
                        last = dve.tensor_scalar(act_raw[:, b * D:(b + 1) * D].rearrange("p (a f) -> p a f", a=1),
                                                 x_sb[:, ds(GB * q + b, 1), :],
                                                 lnscale[:, b:b + 1], lnbias[:, b:b + 1], ALU.mult, ALU.add)
                    last.then_inc(normed, 1)

            def first_aggr(i):
                dve.wait_ge(stats0_ready, i + 1)
                for b in range(i * XP, (i + 1) * XP):
                    last = dve.bn_aggr(mv0[:, b, :], stats0[:, b, :])
                last.then_inc(mv0_ready, 1)

            def first_affine(i):
                cols = slice(i * XP, (i + 1) * XP)
                dve.wait_ge(std0_ready, i + 1)
                dve.reciprocal(rstd0[:, cols], std0[:, cols]).then_inc(rstd0_ready, 1)
                dve.wait_ge(rstd0_ready, i + 1)
                dve.scalar_tensor_tensor(out=bias0[:, cols], in0=mv0[:, cols, 0], scalar=-1.0, in1=rstd0[:, cols],
                                         op0=ALU.mult, op1=ALU.mult).then_inc(bias0_ready, 1)

            def first_stats(i):
                dve.wait_ge(x_in[i], 16)
                for b in range(i * XP, (i + 1) * XP):
                    last = dve.bn_stats(stats0[:, b, :], x_sb[:, b, :])
                last.then_inc(stats0_ready, 1)
                first_aggr(i)

            def load_hc0(j):
                dve.wait_ge(h_ready, j // 2 + 1)
                for dst, src in ((hc_hi, h_hi[0]), (hc_lo, h_lo[0])):
                    dve.tensor_copy(dst[:, 2 * j:2 * j + 2, :], src[:, 2 * j:2 * j + 2, :].bitcast(F32)).then_inc(hc_ready, 1)

            def turn_out(c, g, k):
                s = (c * NG + g) * CB + k
                dve.wait_ge(at_hi_done, s + 1)
                if k not in ACT_RAW:
                    if k % 2 == 0 and not (isinstance(c, int) and c == 0 and g == 0):
                        dve.wait_ge(stored[k // 2], 16 * (c * NG + g))
                    dve.tensor_copy(at_raw_block(k), turn_ps[k % 4][:, :])
                dve.tensor_tensor(atb(a_lo, k), turn_ps[k % 4][:, :], atb(a_hi, k).bitcast(F32), ALU.subtract)\
                   .then_inc(at_lo_done, 1)

            def row_out(c, g):
                u = c * NG + g
                dve.wait_ge(at_free, 4 + (u + 1) * CB)
                dve.tensor_tensor(acc[:, g * GW:(g + 1) * GW], row_ps[g % 2][:, :], acc[:, g * GW:(g + 1) * GW],
                                  ALU.add).then_inc(row_free, 1)

            def link(ins, n):
                ins.then_inc(deg_step, 1)
                dve.wait_ge(deg_step, n)

            def inverse_degree(dst, part, start):
                link(dve.tensor_reduce(deg[:, 0, :], part, AX_X, ALU.add), start + 1)
                dve.tensor_scalar(deg[:, 1, :], deg[:, 0, :], 0.0, None, ALU.max).then_inc(deg_step, 1)
                link(dve.tensor_scalar(deg[:, 2, :], deg[:, 0, :], 0.0, None, ALU.is_le), start + 3)
                link(dve.tensor_tensor(deg[:, 3, :], deg[:, 1, :], deg[:, 2, :], ALU.add), start + 4)
                link(dve.reciprocal(dst, deg[:, 3, :]), start + 5)

            def add_scaled(zi, bank, block0, inv):
                dve.wait_ge(z_ready, zi + 1)
                if not (isinstance(zi, int) and zi == 0):
                    dve.wait_ge(z_free, zi)
                for b in range(GB):
                    last = dve.scalar_tensor_tensor(out=x_sb[:, ds(block0 + b, 1), :],
                                                    in0=row_ps[bank][:, b * D:(b + 1) * D].rearrange("p (a f) -> p a f", a=1),
                                                    scalar=inv[:, ds(block0 + b, 1)],
                                                    in1=x_sb[:, ds(block0 + b, 1), :],
                                                    op0=ALU.mult, op1=ALU.add)
                last.then_inc(z_free, 1)

            def column_degrees(c, half):
                inverse_degree(inv_col[:, ds(CB * c + GB * half, GB)],
                               col_part[:, ds(CB * c + GB * half, GB), :], DEG_COL * c + 5 * half)

            def group_out(g):
                dve.wait_ge(nat_hi_done, ((NCH - 1) * NG + g + 1) * GB)
                inverse_degree(inv_row[:, GB * g:GB * g + GB], row_part[:, GB * g:GB * g + GB, :],
                               (NCH - 1) * DEG_COL + g * DEG_ROW)
                add_scaled(Z_ROW + g, g % 2, GB * g, inv_row)

            def sweep0(c, first, last):
                for g in range(NG):
                    for k in range(CB):
                        turn_out(c, g, k)
                        if first and (g, k) in FIRST_STATS:
                            first_stats(FIRST_STATS.index((g, k)) + 1)
                        if first and (g, k) in FIRST_AFFINE:
                            first_affine(FIRST_AFFINE.index((g, k)) + 1)
                        if first and g == 0 and k in (0, 1, 4, 5):
                            load_hc0(k if k < 2 else k - 2)
                        if k == 3:
                            if g >= 1:
                                row_out(c, g - 1)
                            elif not first:
                                row_out(c - 1, NG - 1)
                        if not first and g == 0 and k in (4, 5):
                            column_degrees(c - 1, k - 4)
                        if not first and (g, k) in ((0, 7), (1, 1)):
                            half = g
                            add_scaled(2 * (c - 1) + half, 1, CB * (c - 1) + GB * half, inv_col)
                        if last and g >= 2 and k == 1:
                            dve.wait_ge(z_free, Z_ROW + g - 1)
                            ln_stats(0, g - 2)
                        if last and g >= 2 and k == 5:
                            ln_affine(0, g - 2)
                        if last and g >= 1 and k == 7:
                            group_out(g - 1)

            first_stats(0)
            first_affine(0)
            dve.wait_ge(acc_clear, 1)
            sweep0(0, True, False)
            with dve.Fori(1, NCH - 1) as c:
                sweep0(c, False, False)
            sweep0(NCH - 1, False, True)

            def finish_sweep0(s):
                if s == 0:
                    row_out(NCH - 1, NG - 1)
                if s == 4:
                    group_out(NG - 1)
                if s in (5, 6):
                    half = s - 5
                    inverse_degree(inv_col[:, NB - CB + GB * half:NB - CB + GB * half + GB],
                                   col_part[:, NB - CB + GB * half:NB - CB + GB * half + GB, :],
                                   (NCH - 1) * DEG_COL + NG * DEG_ROW + 5 * half)
                if s in (6, 7):
                    add_scaled(Z0 - 2 + s - 6, s - 6, NB - CB + GB * (s - 6), inv_col)
                for i, q in enumerate((NG - 2, NG - 1)):
                    if s == 8 + 2 * i:
                        dve.wait_ge(z_free, Z0)
                        ln_stats(0, q)
                    if s == 9 + 2 * i:
                        ln_affine(0, q)
                if s == 14:
                    dve.tensor_reduce(deg_sum[:, :], row_part[:, :, :], AX_X, ALU.add).then_inc(deg_step, 1)
                    dve.wait_ge(deg_step, DEG_ALL - 1)
                    dve.tensor_scalar(d_isqrt[:, :], deg_sum[:, :], 1.0, None, ALU.add).then_inc(deg_step, 1)
                if s == 15:
                    dve.wait_ge(dsq_ready, 1)
                    dve.reciprocal(d_isqrt[:, :], d_isqrt[:, :]).then_inc(dsq_ready, 1)
                    dve.wait_ge(dsq_ready, 2)

            def z_out(sweep, q, par):
                g = (sweep - 1) * NG + q
                bias = b_sb[:, B_OF[sweep]:B_OF[sweep] + 1, :].to_broadcast([P, GB, D])
                dve.wait_ge(z_ready, Z0 + g + 1)
                z4 = z_ps[par][:, :].rearrange("p (b f) -> p b f", b=GB)
                zt4 = zt[:, :].rearrange("p (b f) -> p b f", b=GB)
                if sweep in (1, 2):
                    if sweep == 1 and not (isinstance(q, int) and q == 0):
                        dve.wait_ge(act_ready, SPLIT_BEFORE[1] + q)
                    if sweep == 2 and isinstance(q, int) and q == 0:
                        dve.wait_ge(act_ready, SPLIT_BEFORE[1] + NG)
                    dve.tensor_tensor(zt4, z4, bias, ALU.add).then_inc(zt_ready, 1)
                else:
                    for b in range(GB):
                        last = dve.scalar_tensor_tensor(out=zt[:, b * D:(b + 1) * D], in0=z_ps[par][:, b * D:(b + 1) * D],
                                                        scalar=d_isqrt[:, ds(GB * q + b, 1)],
                                                        in1=b_sb[:, B_OF[sweep], :], op0=ALU.mult, op1=ALU.add)
                    last.then_inc(zt_ready, 1)
                    dve.wait_ge(zt_ready, 2 + ZT_BEFORE[sweep] + q + 1)
                    dve.scalar_tensor_tensor(out=x_sb[:, ds(GB * q, GB), :], in0=zt4, scalar=0.0,
                                             in1=x_sb[:, ds(GB * q, GB), :], op0=ALU.max, op1=ALU.add)\
                       .then_inc(x_upd, 1)

            def group(sweep, q, odd):
                ps, pq = before(sweep, q)
                for s in range(NS):
                    sidx = ((sweep - 1) * NG + q) * NS + s
                    if s not in POOL_LO:
                        dve.wait_ge(sub_hi, sidx + 1)
                        dve.tensor_tensor(sub(a_lo, s), sub_raw(sweep, q, s), sub(a_hi, s).bitcast(F32), ALU.subtract)\
                           .then_inc(sub_lo, 2 if s - 1 in POOL_LO else 1)
                    if ps == 0:
                        finish_sweep0(s)
                        continue
                    if s == AT_Z:
                        z_out(ps, pq, 1 - odd)
                    if s == AT_STATS[ps]:
                        if ps == 2:
                            x_plus_silu(pq)
                        dve.wait_ge(x_upd, XUPD_BEFORE[ps] + pq + 1)
                        ln_stats(ps, pq)
                    if s == AT_AFFINE[ps]:
                        ln_affine(ps, pq)

            def x_plus_silu(q):
                dve.wait_ge(silu_ready, q + 1)
                zt4 = zt[:, :].rearrange("p (b f) -> p b f", b=GB)
                dve.tensor_tensor(x_sb[:, ds(GB * q, GB), :], zt4, x_sb[:, ds(GB * q, GB), :], ALU.add)\
                   .then_inc(x_upd, 1)

            for sweep in range(1, SWEEPS + 1):
                run_groups(dve, sweep, group)
            z_out(SWEEPS, NG - 1, 1)

        @block.tensor
        def _(pe):
            pe.wait_ge(ident_made, 3)

            def split_products(ps, hi_w, lo_w, hi_a, lo_a, start, stop):
                pe.matmul(ps, hi_w, hi_a, start=start, stop=False)
                pe.matmul(ps, lo_w, hi_a, start=False, stop=False)
                return pe.matmul(ps, hi_w, lo_a, start=False, stop=stop)

            def weight_product(ps, src, w):
                for b in range(GB):
                    last = pe.matmul(ps[:, b * D:(b + 1) * D], src[:, b * P:(b + 1) * P], w_sb[:, w, :],
                                     start=True, stop=True)
                last.then_inc(z_ready, 1)

            LEAD = 3

            def turn(c, g, k):
                s = (c * NG + g) * CB + k
                if k == 0:
                    for a in range(GB):
                        pe.wait_ge(nat_in[4 * (g % 2) + a], 16 * (c * (NG // 2) + g // 2) + 16)
                if not (isinstance(s, int) and s < 4):
                    pe.wait_ge(at_lo_done, s - 3)
                for a in range(GB):
                    last = pe.transpose(turn_ps[k % 4][:, a * P:(a + 1) * P], nat_raw(g, a)[:, k * P:(k + 1) * P],
                                        ident[:, :])
                last.then_inc(turned, 1)

            def col_product(c, g, k):
                a, half = k // 2, k % 2
                n = (c * NG + g) * GB + a
                if isinstance(c, int) and c == 0 and k == 0:
                    pe.wait_ge(h_ready, g + 1)
                if g == 0 and k == 0:
                    pe.wait_ge(col_free, c + 1)
                if half == 0:
                    pe.wait_ge(nat_lo_done, n + 1)
                cols = slice(half * GW, (half + 1) * GW)
                last = split_products(col_ps[half][:, :], h_hi[0][:, GB * g + a, :], h_lo[0][:, GB * g + a, :],
                                      nat(a_hi, a)[:, cols], nat(a_lo, a)[:, cols],
                                      g == 0 and a == 0, g == NG - 1 and a == GB - 1)
                if half == 1:
                    last.then_inc(nat_free, 1)

            def row_product(c, g, k):
                s = (c * NG + g) * CB + k
                if k == 0:
                    pe.wait_ge(row_free, c * NG + g + 1)
                if g == 0 and k % 2 == 0:
                    pe.wait_ge(hc_ready, c * CB + k + 2)
                pe.wait_ge(at_lo_done, s + 1)
                last = split_products(row_ps[g % 2][:, :], hc_hi[:, k, :], hc_lo[:, k, :],
                                      atb(a_hi, k), atb(a_lo, k), k == 0, k == CB - 1)
                last.then_inc(at_free, 1)

            def row_weights(g):
                pe.wait_ge(row_free, 2 + (NCH - 1) * NG + g + 1)
                weight_product(row_ps[g % 2], acc[:, g * GW:(g + 1) * GW], 0)

            def sweep0(c, first, last):
                for g in range(NG):
                    for k in range(CB):
                        ahead = g * CB + k + LEAD
                        if not (last and ahead >= NG * CB):
                            turn(c + ahead // (NG * CB), ahead // CB % NG, ahead % CB)
                        col_product(c, g, k)
                        if last and g >= 2 and k == 0:
                            pe.wait_ge(z_free, Z_ROW + g - 1)
                        if not first and g == 1 and k == 0:
                            pe.wait_ge(z_free, 2 * c)
                        row_product(c, g, k)
                        if last and g >= 1 and k == 3:
                            row_weights(g - 1)
                        if not first and g == 0 and k in (3, 6):
                            half = k // 6
                            if half == 0:
                                pe.wait_ge(row_free, 2 + c * NG)
                                pe.wait_ge(col_free, c + 1)
                            else:
                                pe.wait_ge(z_free, 2 * c - 1)
                            weight_product(row_ps[1], prod_t[:, half, :], 1)

            for k in range(LEAD):
                turn(0, 0, k)
            sweep0(0, True, False)
            pe.wait_ge(const_in, 16 * 8)
            with pe.Fori(1, NCH - 1) as c:
                sweep0(c, False, False)
            sweep0(NCH - 1, False, True)

            def finish_sweep0(s):
                if s == 1:
                    row_weights(NG - 1)
                if s == 2:
                    pe.wait_ge(col_free, NCH + 1)
                    pe.wait_ge(z_free, Z0 - 3)
                    weight_product(row_ps[0], prod_t[:, 0, :], 1)
                if s == 4:
                    pe.wait_ge(z_free, Z0 - 2)
                    weight_product(row_ps[1], prod_t[:, 1, :], 1)

            def group(sweep, q, odd):
                s_in = SET_OF[sweep - 1]
                hi, lo = h_hi[s_in], h_lo[s_in]
                ps, pq = before(sweep, q)
                gidx = (sweep - 1) * NG + q
                bank = prod_ps[odd][:, :]
                first_group = isinstance(q, int) and q == 0
                if sweep == 1 and first_group:
                    pe.wait_ge(at_lo_done, STEPS)
                pe.wait_ge(prod_free, gidx + 1)
                for s in range(NS):
                    sidx = gidx * NS + s
                    if first_group and s % 2 == 0:
                        pe.wait_ge(h_ready, SPLIT_BEFORE[sweep - 1] + s // 2 + 1)
                    pe.wait_ge(sub_hi, sidx + 1)
                    for b in range(SB2):
                        cols = slice(b * GW, (b + 1) * GW)
                        pe.matmul(bank, hi[:, SB2 * s + b, :], sub(a_hi, s)[:, cols], start=(s == 0 and b == 0), stop=False)
                        pe.matmul(bank, lo[:, SB2 * s + b, :], sub(a_hi, s)[:, cols], start=False, stop=False)
                    if s in POOL_LO:
                        pe.wait_ge(sub_lo_pool, gidx * NS + POOL_INC * (POOL_LO.index(s) + 1))
                    else:
                        pe.wait_ge(sub_lo, sidx + 1)
                    for b in range(SB2):
                        cols = slice(b * GW, (b + 1) * GW)
                        last = pe.matmul(bank, hi[:, SB2 * s + b, :], sub(a_lo, s)[:, cols], start=False,
                                         stop=(s == NS - 1 and b == SB2 - 1))
                    last.then_inc(sub_used, 1)
                    if s == NS - 3 and sweep >= 3:
                        identity_product(sweep, q, bank)
                    if ps == 0:
                        finish_sweep0(s)
                    if s == AT_WEIGHTS and ps > 0:
                        finish(ps, pq, 1 - odd)

            def identity_product(sweep, q, bank):
                pe.wait_ge(hd_ready, 2 * ((sweep - 3) * NG + q) + 2)
                for b in range(GB):
                    for part in (hd_hi, hd_lo):
                        pe.matmul(bank[:, b * P:(b + 1) * P], part[:, b, :], ident_r[:, :], start=False, stop=False,
                                  skip_group_check=True)

            def finish(sweep, q, par):
                g = (sweep - 1) * NG + q
                pe.wait_ge(prod_free, 2 + g + 1)
                pe.wait_ge(zt_ready, g + 1)
                weight_product(z_ps[par], prod_t[:, par, :], W_OF[sweep])

            for sweep in range(1, SWEEPS + 1):
                run_groups(pe, sweep, group)
            finish(SWEEPS, NG - 1, 1)


_INS = ['x', 'adj', 'L0_gnn_W_in', 'L0_gnn_W_out', 'L1_gnn_W', 'L1_gnn_b', 'L2_gnn_W', 'L2_gnn_b',
        'L3_gnn_W', 'L3_gnn_b']
_OUTS = [((4096, 128), 'float32')]


def kernel(**inputs):
    import numpy as _np
    import concourse.bacc as _bacc
    from concourse import mybir as _mybir
    from concourse.bass_utils import run_bass_kernel_spmd as _run

    nc = _bacc.Bacc("TRN2", target_bir_lowering=False, num_devices=1)
    arrays, args = {}, []
    for name in _INS:
        a = _np.ascontiguousarray(inputs[name])
        arrays[f"in_{name}_dram"] = a
        args.append(nc.dram_tensor(f"in_{name}_dram", a.shape, _mybir.dt.from_np(a.dtype), kind="ExternalInput").ap())
    for i, (shape, dtype) in enumerate(_OUTS):
        dt = _mybir.dt.from_np(_np.dtype(dtype))
        args.append(nc.dram_tensor(f"out_{i}_dram", shape, dt, kind="ExternalOutput").ap())
    build_gnn_stack(nc, *args)
    r = _run(nc, [arrays], core_ids=[0])
    got = tuple(r.results[0][f"out_{i}_dram"] for i in range(len(_OUTS)))
    return got[0]
```

```python
from contextlib import ExitStack

import concourse.bass as bass
from concourse import mybir

F32 = mybir.dt.float32
F32R = mybir.dt.float32r
ALU = mybir.AluOpType
ACT = mybir.ActivationFunctionType
AX_X = mybir.AxisListType.X
ds = bass.ds

P = 128
EPS = 1e-5


def build_gnn_stack(nc, x, adj, w_in, w_out, w1, b1, w2, b2, w3, b3, out):
    N, D = x.shape
    assert D == P and N % 1024 == 0
    NB = N // P
    GB = 4
    GW = GB * P
    NG = N // GW
    CB = 8
    CW = CB * P
    NCH = N // CW
    UNITS = NCH * NG
    STEPS = UNITS * CB
    SUBS = UNITS * GB
    SB2 = 2
    NS = NB // SB2
    NT = NS // 2
    SWEEPS = 4
    Z0 = 2 * NG
    Z_ROW = 2 * (NCH - 1)
    FIRST_STATS, FIRST_STD, FIRST_AFFINE = [(0, 2), (1, 5), (3, 5)], [(0, 6), (1, 7), (3, 7)], [(0, 7), (2, 1), (4, 1)]
    POOL_LO = {0: 4, 6: 8, 8: 12, 12: 16}
    ACT_RAW = (3, 7)

    adj_t = nc.dram_tensor("adj_t_scratch", (NG, P, NB * GW), F32, kind="Internal").ap()

    ctx = ExitStack()
    with ctx:
        def sb(name, shape, dt=F32):
            return ctx.enter_context(nc.sbuf_tensor(name, shape, dt))

        def sem(name):
            return ctx.enter_context(nc.semaphore(name))

        x_sb = sb("x_sb", [P, NB, D])
        h_hi = [sb(f"h_hi{i}", [P, NB, D], F32R) for i in range(2)]
        h_lo = [sb(f"h_lo{i}", [P, NB, D], F32R) for i in range(2)]
        raw = sb("raw", [P, 8, 1024])
        a_hi = sb("a_hi", [P, 6, 1024], F32R)
        a_lo = sb("a_lo", [P, 6, 1024], F32R)
        keep = sb("keep", [P, NG, 1024])
        acc = keep[:, 0:4, :].rearrange("p a n -> p (a n)")
        at_raw = keep[:, 4:8, :]
        prod_t = sb("prod_t", [P, 2, GW])
        w_sb = sb("w_sb", [P, 5, D])
        b_sb = sb("b_sb", [P, 3, D])
        ident = sb("ident", [P, P])
        ident_r = sb("ident_r", [P, P], F32R)
        row_part = sb("row_part", [P, NB, NCH])
        col_part = sb("col_part", [P, NB, NG])
        deg = sb("deg", [P, 4, GB])
        deg_sum = sb("deg_sum", [P, NB])
        inv_row = sb("inv_row", [P, NB])
        inv_col = sb("inv_col", [P, NB])
        d_isqrt = sb("d_isqrt", [P, NB])
        zt = sb("zt", [P, GW])
        act_raw = sb("act_raw", [P, GW])
        stats = sb("stats", [P, GB, 6])
        mv = sb("mv", [P, GB, 2])
        std = sb("std", [P, GB])
        rstd = sb("rstd", [P, GB])
        lnscale = sb("lnscale", [P, GB])
        lnbias = sb("lnbias", [P, GB])
        carrier = sb("carrier", [P, 1])
        table_warm = sb("table_warm", [P, 1])
        eps_sb = sb("eps_sb", [P, 1])
        minus_half = sb("minus_half", [P, 1])
        newton = sb("newton", [P, 3, GB])

        banks = [ctx.enter_context(nc.psum_tensor(f"bank{i}", [P, 512], F32)) for i in range(8)]
        turn_ps = banks[0:2] + banks[6:8]
        row_ps, col_ps = banks[2:4], banks[4:6]
        z_ps = banks[6:8]
        prod_ps = banks[0:2]

        hc_hi, hc_lo = h_hi[1][:, NB - CB:NB, :], h_lo[1][:, NB - CB:NB, :]
        hd_hi = a_hi[:, 4, 0:GW].rearrange("p (b f) -> p b f", b=GB)
        hd_lo = a_lo[:, 4, 0:GW].rearrange("p (b f) -> p b f", b=GB)

        XP = NB // 4
        stats0 = zt[:, 0:6 * NB].rearrange("p (b s) -> p b s", s=6)
        mv0 = zt[:, 256:256 + 2 * NB].rearrange("p (b s) -> p b s", s=2)
        std0, rstd0, bias0 = (zt[:, 384 + i * NB:384 + (i + 1) * NB] for i in range(3))

        def at_raw_block(k):
            return at_raw[:, k // 2, (k % 2) * GW:(k % 2 + 1) * GW]

        def nat_raw(u, a):
            return raw[:, 4 * (u % 2) + a, :]

        def nat(t, a):
            return t[:, a, :]

        def atb(t, k):
            k = k % 4
            return t[:, 4 + k // 2, (k % 2) * GW:(k % 2 + 1) * GW]

        def sub_raw(sweep, q, s):
            if s == NS - 1:
                return keep[:, ds(q, 1), :].rearrange("p a n -> p (a n)")
            return raw[:, s % 8, :]

        def sub(t, s):
            return t[:, s % 4, :]

        x_in = [sem(f"x_in{i}") for i in range(4)]
        stats0_ready = sem("stats0_ready")
        mv0_ready = sem("mv0_ready")
        std0_ready = sem("std0_ready")
        rstd0_ready = sem("rstd0_ready")
        bias0_ready = sem("bias0_ready")
        const_in = sem("const_in")
        ident_made = sem("ident_made")
        eps_made = sem("eps_made")
        nat_in = [sem(f"nat_in{i}") for i in range(8)]
        tile_in = [sem(f"tile_in{i}") for i in range(4)]
        stored = [sem(f"stored{i}") for i in range(4)]
        kept_in = sem("kept_in")
        turned = sem("turned")
        at_hi_done = sem("at_hi_done")
        at_lo_done = sem("at_lo_done")
        at_free = sem("at_free")
        nat_hi_done = sem("nat_hi_done")
        nat_lo_done = sem("nat_lo_done")
        nat_free = sem("nat_free")
        row_free = sem("row_free")
        col_free = sem("col_free")
        acc_clear = sem("acc_clear")
        hc_ready = sem("hc_ready")
        z_ready = sem("z_ready")
        z_free = sem("z_free")
        sub_hi = sem("sub_hi")
        sub_lo = sem("sub_lo")
        sub_lo_pool = sem("sub_lo_pool")
        sub_used = sem("sub_used")
        prod_free = sem("prod_free")
        hd_ready = sem("hd_ready")
        zt_ready = sem("zt_ready")
        silu_ready = sem("silu_ready")
        x_upd = sem("x_upd")
        stats_ready = sem("stats_ready")
        mv_ready = sem("mv_ready")
        std_ready = sem("std_ready")
        rstd_ready = sem("rstd_ready")
        lnscale_ready = sem("lnscale_ready")
        lnbias_ready = sem("lnbias_ready")
        newton_done = sem("newton_done")
        normed = sem("normed")
        act_ready = sem("act_ready")
        h_hi_ready = sem("h_hi_ready")
        h_ready = sem("h_ready")
        deg_step = sem("deg_step")
        dsq_ready = sem("dsq_ready")
        out_done = sem("out_done")

        LN_BEFORE = {0: 0, 2: NG, 3: 2 * NG}
        SPLIT_BEFORE = {-1: 0, 0: NG, 1: 2 * NG, 2: 3 * NG, 3: 4 * NG}
        XUPD_BEFORE = {2: 0, 3: NG, 4: 2 * NG}
        ZT_BEFORE = {1: 0, 2: NG, 3: 2 * NG, 4: 3 * NG}
        SET_OF = {-1: 0, 0: 1, 1: 0, 2: 1, 3: 0}
        W_OF = {1: 2, 2: 2, 3: 3, 4: 4}
        B_OF = {1: 0, 2: 0, 3: 1, 4: 2}

        DEG_COL = 5 * 2
        DEG_ROW = 5
        DEG_ALL = NCH * DEG_COL + NG * DEG_ROW + 2

        def run_groups(eng, sweep, group):
            group(sweep, 0, 0)
            with eng.Fori(0, (NG - 2) // 2) as m:
                group(sweep, 2 * m + 1, 1)
                group(sweep, 2 * m + 2, 0)
            group(sweep, NG - 1, 1)

        TW = 2048

        AT_PROD, AT_WEIGHTS, AT_Z, AT_SILU = 3, 1, 6, 7
        AT_STATS = {1: None, 2: 8, 3: 8, 4: None}
        AT_RSTD = 10
        AT_OWN = 5
        LAST_TWO = (6, 8, 8, 9, 10), (9, 10, 11, 12, 13)
        AT_AFFINE = {1: None, 2: 12, 3: 12, 4: None}
        AT_NORM = {1: None, 2: 12, 3: 12, 4: None}
        AT_HI = {1: 9, 2: 13, 3: 13, 4: None}

        def pool_lo_count(sweep, q, t):
            group, tile = (sweep - 1) * NG + q + (t - 4) // NT, (t - 4) % NT
            return group * NS + POOL_LO[2 * tile] if 2 * tile in POOL_LO else None

        def normed_by_vector(sweep, q):
            return sweep in (2, 3) or sweep == 0 and q >= NG - 2

        def before(sweep, q):
            if isinstance(q, int) and q == 0:
                return sweep - 1, NG - 1
            return sweep, q - 1

        block = ctx.enter_context(nc.Block())

        @block.sync
        def _(sp):
            xv = x.rearrange("(b p) d -> p b d", p=P)

            def load_x(i):
                sp.dma_start(x_sb[:, i * XP:(i + 1) * XP, :], xv[:, i * XP:(i + 1) * XP, :]).then_inc(x_in[i], 16)

            def load_nat(c, g):
                for a in range(GB):
                    sp.dma_start(nat_raw(g, a), adj[(GB * g + a) * P:(GB * g + a + 1) * P, ds(c * CW, CW)])\
                      .then_inc(nat_in[4 * (g % 2) + a], 16)

            load_x(0)
            load_nat(0, 0)
            load_x(1)
            load_nat(0, 1)
            for i in (2, 3):
                load_x(i)
            for i, w in enumerate((w_in, w_out, w1, w2, w3)):
                sp.dma_start(w_sb[:, i, :], w).then_inc(const_in, 16)
            for i, b in enumerate((b1, b2, b3)):
                sp.dma_start(b_sb[:, i, :], b.rearrange("(a n) -> a n", a=1).to_broadcast([P, D])).then_inc(const_in, 16)

            def load_tile(sweep, q, t):
                width = TW // 2 if t == NT - 1 else TW
                sp.dma_start(raw[:, 2 * (t % 4):2 * (t % 4) + 2, :].rearrange("p a n -> p (a n)")[:, 0:width],
                             adj_t[q, :, t * TW:t * TW + width]).then_inc(tile_in[t % 4], 16)

            def store(c, g, j):
                sp.wait_ge(at_lo_done, c * NG * CB + g * CB + 2 * j + 2)
                sp.dma_start(adj_t[g, :, ds(c * CB * GW + 2 * j * GW, 2 * GW)],
                             at_raw[:, j, :]).then_inc(stored[j], 16)

            def sweep0(c, last):
                for g in range(NG):
                    for j in range(3):
                        store(c, g, j)
                    sp.wait_ge(turned, (c * NG + g) * CB + CB)
                    sp.wait_ge(nat_lo_done, (c * NG + g) * GB + GB)
                    if not (last and g >= NG - 2):
                        load_nat(c + (g + 2) // NG, (g + 2) % NG)
                    else:
                        if g == NG - 2:
                            for j in range(4):
                                sp.wait_ge(stored[j], 16 * ((NCH - 1) * NG + 1))
                        for t in range(2):
                            load_tile(1, 0, 2 * (g % 2) + t)
                    if not (last and g == NG - 1):
                        store(c, g, 3)

            with sp.Fori(0, NCH - 1) as c:
                sweep0(c, False)
            sweep0(NCH - 1, True)

            def load_tiles(sweep, q):
                first_group = isinstance(q, int) and q == 0
                for t in range(NT):
                    if sweep == 1 and first_group and t < 4:
                        continue
                    by_pool = pool_lo_count(sweep, q, t)
                    if by_pool is not None:
                        sp.wait_ge(sub_lo_pool, by_pool)
                    sp.wait_ge(sub_lo, ((sweep - 1) * NG * NT + q * NT + t - 4) * 2 + 2)
                    load_tile(sweep, q, t)
                if sweep == 1 and not (isinstance(q, int) and q == NG - 1):
                    if first_group:
                        sp.wait_ge(z_ready, Z0 - 2)
                    sp.dma_start(keep[:, ds(q, 1), :].rearrange("p a n -> p (a n)"), adj_t[q, :, N * GB - 1024:N * GB])\
                      .then_inc(kept_in, 16)

            for sweep in range(1, SWEEPS + 1):
                load_tiles(sweep, 0)
                if sweep == 1:
                    for j in range(4):
                        sp.wait_ge(stored[j], 16 * (UNITS - (1 if j == 3 else 0)))
                load_tiles(sweep, 1)
                with sp.Fori(2, NG - 1) as q:
                    load_tiles(sweep, q)
                load_tiles(sweep, NG - 1)

            with sp.Fori(0, NG) as q:
                sp.wait_ge(x_upd, XUPD_BEFORE[4] + q + 1)
                sp.dma_start(out.rearrange("(g b p) d -> g p b d", p=P, b=GB)[q], x_sb[:, ds(GB * q, GB), :])\
                  .then_inc(out_done, 16)
            sp.wait_ge(out_done, 16 * NG)

        @block.gpsimd
        def _(pool):
            pool.memset(ident[:, :], 0.0).then_inc(ident_made, 1)
            pool.memset(eps_sb[:, :], EPS).then_inc(eps_made, 1)
            pool.memset(minus_half[:, :], -0.5)
            pool.wait_ge(ident_made, 1)
            pool.affine_select(out=ident[:, :], in_=ident[:, :], compare_op=ALU.not_equal, fill=1.0,
                               base=0, pattern=[[-1, P]], channel_multiplier=1).then_inc(ident_made, 1)

            def split_lo(sweep, q):
                s = SET_OF[sweep]
                pool.wait_ge(h_hi_ready, SPLIT_BEFORE[sweep] + q + 1)
                pool.tensor_tensor(h_lo[s][:, ds(GB * q, GB), :],
                                   act_raw[:, :].rearrange("p (b f) -> p b f", b=GB),
                                   h_hi[s][:, ds(GB * q, GB), :].bitcast(F32), ALU.subtract).then_inc(h_ready, 1)

            def nat_split(c, g, a):
                n = (c * NG + g) * GB + a
                pool.wait_ge(nat_hi_done, n + 1)
                pool.tensor_tensor(nat(a_lo, a), nat_raw(g, a), nat(a_hi, a).bitcast(F32),
                                   ALU.subtract).then_inc(nat_lo_done, 1)

            def load_hc(c, j):
                pool.wait_ge(at_free, 4 + c * NG * CB - CB + 2 * j + 2)
                for dst, src in ((hc_hi, h_hi[0]), (hc_lo, h_lo[0])):
                    pool.tensor_copy(dst[:, 2 * j:2 * j + 2, :], src[:, ds(CB * c + 2 * j, 2), :].bitcast(F32))\
                        .then_inc(hc_ready, 1)

            def sweep0(c, first, last):
                for g in range(NG):
                    for a in range(GB):
                        if last and a == 1 and g >= 3:
                            split_lo(0, g - 3)
                        nat_split(c, g, a)
                        if not first and g == 0 and a < 2:
                            load_hc(c, 2 + a)
                        if first and a == 2 and g < NG - 1:
                            split_lo(-1, g + 1)
                        if not last and g == NG - 1 and a >= 2:
                            load_hc(c + 1, a - 2)

            split_lo(-1, 0)
            sweep0(0, True, False)
            with pool.Fori(1, NCH - 1) as c:
                sweep0(c, False, False)
            sweep0(NCH - 1, False, True)
            split_lo(0, NG - 3)

            def pool_rstd(n):
                pool.wait_ge(mv_ready, n + 1)
                pool.tensor_tensor(std[:, :], mv[:, :, 1], eps_sb[:, :].to_broadcast([P, GB]), ALU.add)\
                    .then_inc(std_ready, 1)
                pool.wait_ge(std_ready, n + 1)
                pool.tensor_tensor(rstd[:, :], std[:, :], minus_half[:, :].to_broadcast([P, GB]), ALU.pow)\
                    .then_inc(rstd_ready, 1)

            def sub_split(sweep, q, s):
                g = (sweep - 1) * NG + q
                pool.wait_ge(sub_hi, g * NS + s + 1)
                pool.tensor_tensor(sub(a_lo, s), sub_raw(sweep, q, s), sub(a_hi, s).bitcast(F32), ALU.subtract)\
                    .then_inc(sub_lo_pool, POOL_LO[s] - max([0] + [POOL_LO[r] for r in POOL_LO if r < s]))

            def group(sweep, q, odd):
                sub_split(sweep, q, min(POOL_LO))
                ps, pq = before(sweep, q)
                for s in sorted(POOL_LO)[1:]:
                    if s > AT_RSTD and ps in (2, 3):
                        pool_rstd(LN_BEFORE[ps] + pq)
                    if s > AT_RSTD and ps == 0:
                        split_lo(0, NG - 2)
                    sub_split(sweep, q, s)
                if ps == 0:
                    split_lo(0, NG - 1)
                if 1 <= ps <= 3:
                    split_lo(ps, pq)

            for sweep in range(1, SWEEPS + 1):
                run_groups(pool, sweep, group)

        @block.scalar
        def _(act):
            act.wait_ge(eps_made, 1)
            act.activation(table_warm[:, :], eps_sb[:, :], ACT.Sqrt)
            act.wait_ge(ident_made, 2)
            act.activation(ident_r[:, :], ident[:, :], ACT.Copy).then_inc(ident_made, 1)

            def first_std(i):
                act.wait_ge(mv0_ready, i + 1)
                act.activation(std0[:, i * XP:(i + 1) * XP], mv0[:, i * XP:(i + 1) * XP, 1], ACT.Sqrt,
                               bias=eps_sb[:, 0:1]).then_inc(std0_ready, 1)

            def ln_std(n):
                act.wait_ge(mv_ready, n + 1)
                act.activation(std[:, :], mv[:, :, 1], ACT.Sqrt, bias=eps_sb[:, 0:1]).then_inc(std_ready, 1)

            def split_hi(sweep, q):
                m = SPLIT_BEFORE[sweep] + q
                if normed_by_vector(sweep, q):
                    act.wait_ge(normed, LN_BEFORE[sweep] + q - (NG - 2) + 1)
                    act.activation(act_raw[:, :], act_raw[:, :], ACT.Relu).then_inc(act_ready, 1)
                act.wait_ge(act_ready, m + 1)
                act.activation(h_hi[SET_OF[sweep]][:, ds(GB * q, GB), :],
                               act_raw[:, :].rearrange("p (b f) -> p b f", b=GB),
                               ACT.Copy).then_inc(h_hi_ready, 1)

            def ln_relu(sweep, q):
                n, m = LN_BEFORE[sweep] + q, SPLIT_BEFORE[sweep] + q
                act.wait_ge(lnbias_ready, n + 1)
                act.wait_ge(h_ready, m)
                for b in range(GB):
                    last = act.activation(act_raw[:, b * D:(b + 1) * D], x_sb[:, GB * q + b, :], ACT.Relu,
                                          bias=lnbias[:, b:b + 1], scale=lnscale[:, b:b + 1])
                last.then_inc(act_ready, 1)
                split_hi(sweep, q)

            def first_relu(q):
                act.wait_ge(bias0_ready, GB * q // XP + 1)
                if q > 0:
                    act.wait_ge(h_ready, q)
                for b in range(GB):
                    n = GB * q + b
                    last = act.activation(act_raw[:, b * D:(b + 1) * D], x_sb[:, n, :], ACT.Relu,
                                          bias=bias0[:, n:n + 1], scale=rstd0[:, n:n + 1])
                last.then_inc(act_ready, 1)
                split_hi(-1, q)

            def nat_hi(c, g, a):
                n = (c * NG + g) * GB + a
                act.wait_ge(nat_in[4 * (g % 2) + a], 16 * (c * (NG // 2) + g // 2) + 16)
                act.wait_ge(nat_free, n + 1)
                act.activation(nat(a_hi, a), nat_raw(g, a), ACT.Copy,
                               accum_out=row_part[:, GB * g + a, ds(c, 1)]).then_inc(nat_hi_done, 1)

            def at_hi(c, g, k):
                s = (c * NG + g) * CB + k
                act.wait_ge(turned, s + 1)
                if k in ACT_RAW:
                    if not (isinstance(c, int) and c == 0 and g == 0):
                        act.wait_ge(stored[k // 2], 16 * (c * NG + g))
                    act.activation(at_raw_block(k), turn_ps[k % 4][:, :], ACT.Copy)
                act.wait_ge(at_free, s + 1)
                act.activation(atb(a_hi, k), turn_ps[k % 4][:, :], ACT.Copy,
                               accum_out=col_part[:, ds(CB * c + k, 1), g]).then_inc(at_hi_done, 1)

            def col_out(c):
                act.wait_ge(nat_free, 4 + (c + 1) * NG * GB)
                for half in range(2):
                    last = act.activation(prod_t[:, half, :], col_ps[half][:, :], ACT.Copy)
                last.then_inc(col_free, 1)

            def sweep0(c, first, last):
                for g in range(NG):
                    for k in range(CB):
                        at_hi(c, g, k)
                        if not first and g == 0 and k == 2:
                            col_out(c - 1)
                        if k % 2 == 0:
                            a = (k // 2 + 1) % GB
                            if a > 0:
                                nat_hi(c, g, a)
                            elif not (last and g == NG - 1):
                                nat_hi(c + (g + 1) // NG, (g + 1) % NG, 0)
                        if first and (g, k) in FIRST_STD:
                            first_std(FIRST_STD.index((g, k)) + 1)
                        if first and g < NG - 1 and k == 3:
                            first_relu(g + 1)
                        if last and g >= 2 and k == 3:
                            ln_std(LN_BEFORE[0] + g - 2)
                        if last and g >= 2 and k == 7:
                            ln_relu(0, g - 2)

            first_std(0)
            first_relu(0)
            nat_hi(0, 0, 0)
            sweep0(0, True, False)
            with act.Fori(1, NCH - 1) as c:
                sweep0(c, False, False)
            sweep0(NCH - 1, False, True)

            def finish_sweep0(s):
                if s == 0:
                    col_out(NCH - 1)
                for half, q in enumerate((NG - 2, NG - 1)):
                    _, at_std, _, _, at_hi_split = LAST_TWO[half]
                    if s == at_std:
                        ln_std(LN_BEFORE[0] + q)
                    if s == at_hi_split:
                        split_hi(0, q)
                if s == 15:
                    act.wait_ge(deg_step, DEG_ALL)
                    act.activation(d_isqrt[:, :], d_isqrt[:, :], ACT.Sqrt).then_inc(dsq_ready, 1)

            def group(sweep, q, odd):
                ps, pq = before(sweep, q)
                for s in range(NS):
                    sidx = ((sweep - 1) * NG + q) * NS + s
                    if s % 2 == 0:
                        act.wait_ge(tile_in[s // 2 % 4], 16 * ((sweep - 1) * NG * 2 + q * 2 + s // 8) + 16)
                    elif s == NS - 1 and sweep == 1 and not (isinstance(q, int) and q == NG - 1):
                        act.wait_ge(kept_in, 16 * q + 16)
                    if sweep == 1 and isinstance(q, int) and q == 0 and s < 4:
                        act.wait_ge(nat_free, SUBS + s + 1)
                    else:
                        act.wait_ge(sub_used, sidx - 3)
                    act.activation(sub(a_hi, s), sub_raw(sweep, q, s), ACT.Copy).then_inc(sub_hi, 1)
                    if ps == 0:
                        finish_sweep0(s)
                        continue
                    if sweep >= 3 and s == AT_OWN:
                        own_input(sweep, q)
                    if s == AT_PROD:
                        prod_out(ps, pq, 1 - odd)
                    if s == AT_SILU and ps in (1, 2):
                        silu(ps, pq)
                    if s == AT_HI[ps]:
                        split_hi(ps, pq)

            def own_input(sweep, q):
                act.wait_ge(h_ready, SPLIT_BEFORE[sweep - 1] + q + 1)
                for dst, src in ((hd_hi, h_hi[SET_OF[sweep - 1]]), (hd_lo, h_lo[SET_OF[sweep - 1]])):
                    act.activation(dst, src[:, ds(GB * q, GB), :], ACT.Copy).then_inc(hd_ready, 1)

            def prod_out(sweep, q, par):
                g = (sweep - 1) * NG + q
                act.wait_ge(sub_used, (g + 1) * NS)
                act.wait_ge(z_ready, Z0 if sweep == 1 and isinstance(q, int) and q == 0 else Z0 + g - 1)
                act.activation(prod_t[:, par, :], prod_ps[par][:, :], ACT.Copy).then_inc(prod_free, 1)

            def silu(sweep, q):
                act.wait_ge(zt_ready, 2 + ZT_BEFORE[sweep] + q + 1)
                if sweep == 1:
                    act.wait_ge(h_ready, SPLIT_BEFORE[1] + q)
                    act.activation(act_raw[:, :], zt[:, :], ACT.Silu).then_inc(act_ready, 1)
                else:
                    act.activation(zt[:, :], zt[:, :], ACT.Silu).then_inc(silu_ready, 1)

            for sweep in range(1, SWEEPS + 1):
                run_groups(act, sweep, group)
            prod_out(SWEEPS, NG - 1, 1)

        @block.vector
        def _(dve):
            def prime(s, n):
                dve.sem_inc(s, n)

            for s, n in ((at_free, 4), (nat_free, 4), (row_free, 2), (col_free, 1), (zt_ready, 2), (prod_free, 2)):
                prime(s, n)

            def carry_wait():
                dve.memset(carrier[:, :], 0.0)

            def ln_stats(sweep, q):
                n = LN_BEFORE[sweep] + q
                carry_wait()
                for b in range(GB):
                    last = dve.bn_stats(stats[:, b, :], x_sb[:, GB * q + b, :])
                last.then_inc(stats_ready, 1)
                dve.wait_ge(stats_ready, n + 1)
                carry_wait()
                for b in range(GB):
                    last = dve.bn_aggr(mv[:, b, :], stats[:, b, :])
                last.then_inc(mv_ready, 1)

            def ln_affine(sweep, q):
                n = LN_BEFORE[sweep] + q
                if sweep == 0:
                    dve.wait_ge(std_ready, n + 1)
                    dve.reciprocal(rstd[:, :], std[:, :]).then_inc(rstd_ready, 1)
                dve.wait_ge(rstd_ready, n + 1)
                if sweep > 0:
                    m = 3 * (n - LN_BEFORE[2])
                    dve.tensor_tensor(newton[:, 0, :], rstd[:, :], rstd[:, :], ALU.mult).then_inc(newton_done, 1)
                    dve.tensor_tensor(newton[:, 1, :], rstd[:, :], d_isqrt[:, ds(GB * q, GB)], ALU.mult)\
                       .then_inc(newton_done, 1)
                    dve.wait_ge(newton_done, m + 1)
                    dve.scalar_tensor_tensor(out=newton[:, 2, :], in0=newton[:, 0, :], scalar=-0.5, in1=std[:, :],
                                             op0=ALU.mult, op1=ALU.mult).then_inc(newton_done, 1)
                    dve.wait_ge(newton_done, m + 3)
                    dve.scalar_tensor_tensor(out=lnscale[:, :], in0=newton[:, 2, :], scalar=1.5, in1=newton[:, 1, :],
                                             op0=ALU.add, op1=ALU.mult).then_inc(lnscale_ready, 1)
                else:
                    dve.tensor_copy(lnscale[:, :], rstd[:, :]).then_inc(lnscale_ready, 1)
                dve.wait_ge(lnscale_ready, n + 1)
                dve.scalar_tensor_tensor(out=lnbias[:, :], in0=mv[:, :, 0], scalar=-1.0, in1=lnscale[:, :],
                                         op0=ALU.mult, op1=ALU.mult).then_inc(lnbias_ready, 1)

            def ln_apply(sweep, q):
                n = LN_BEFORE[sweep] + q
                dve.wait_ge(lnbias_ready, n + 1)
                dve.wait_ge(h_ready, SPLIT_BEFORE[sweep] + q)
                for b in range(GB):
                    last = dve.tensor_scalar(act_raw[:, b * D:(b + 1) * D].rearrange("p (a f) -> p a f", a=1),
                                             x_sb[:, ds(GB * q + b, 1), :],
                                             lnscale[:, b:b + 1], lnbias[:, b:b + 1], ALU.mult, ALU.add)
                last.then_inc(normed, 1)

            dve.memset(acc[:, N - GW:N], 0.0).then_inc(acc_clear, 1)

            def first_aggr(i):
                dve.wait_ge(stats0_ready, i + 1)
                for b in range(i * XP, (i + 1) * XP):
                    last = dve.bn_aggr(mv0[:, b, :], stats0[:, b, :])
                last.then_inc(mv0_ready, 1)

            def first_affine(i):
                cols = slice(i * XP, (i + 1) * XP)
                dve.wait_ge(std0_ready, i + 1)
                dve.reciprocal(rstd0[:, cols], std0[:, cols]).then_inc(rstd0_ready, 1)
                dve.wait_ge(rstd0_ready, i + 1)
                dve.scalar_tensor_tensor(out=bias0[:, cols], in0=mv0[:, cols, 0], scalar=-1.0, in1=rstd0[:, cols],
                                         op0=ALU.mult, op1=ALU.mult).then_inc(bias0_ready, 1)

            def first_stats(i):
                dve.wait_ge(x_in[i], 16)
                for b in range(i * XP, (i + 1) * XP):
                    last = dve.bn_stats(stats0[:, b, :], x_sb[:, b, :])
                last.then_inc(stats0_ready, 1)
                first_aggr(i)

            def load_first_hc(j):
                dve.wait_ge(h_ready, j // 2 + 1)
                for dst, src in ((hc_hi, h_hi[0]), (hc_lo, h_lo[0])):
                    dve.tensor_copy(dst[:, 2 * j:2 * j + 2, :], src[:, 2 * j:2 * j + 2, :].bitcast(F32)).then_inc(hc_ready, 1)

            def turn_out(c, g, k):
                s = (c * NG + g) * CB + k
                dve.wait_ge(at_hi_done, s + 1)
                if k not in ACT_RAW:
                    if k % 2 == 0 and not (isinstance(c, int) and c == 0 and g == 0):
                        dve.wait_ge(stored[k // 2], 16 * (c * NG + g))
                    dve.tensor_copy(at_raw_block(k), turn_ps[k % 4][:, :])
                dve.tensor_tensor(atb(a_lo, k), turn_ps[k % 4][:, :], atb(a_hi, k).bitcast(F32), ALU.subtract)\
                   .then_inc(at_lo_done, 1)

            def row_out(c, g):
                u = c * NG + g
                dve.wait_ge(at_free, 4 + (u + 1) * CB)
                part = acc[:, g * GW:(g + 1) * GW]
                if isinstance(c, int) and c == 0:
                    dve.tensor_copy(part, row_ps[g % 2][:, :]).then_inc(row_free, 1)
                else:
                    dve.tensor_tensor(part, row_ps[g % 2][:, :], part, ALU.add).then_inc(row_free, 1)

            def link(ins, n):
                ins.then_inc(deg_step, 1)
                dve.wait_ge(deg_step, n)

            def inverse_degree(dst, part, start):
                link(dve.tensor_reduce(deg[:, 0, :], part, AX_X, ALU.add), start + 1)
                dve.tensor_scalar(deg[:, 1, :], deg[:, 0, :], 0.0, None, ALU.max).then_inc(deg_step, 1)
                link(dve.tensor_scalar(deg[:, 2, :], deg[:, 0, :], 0.0, None, ALU.is_le), start + 3)
                link(dve.tensor_tensor(deg[:, 3, :], deg[:, 1, :], deg[:, 2, :], ALU.add), start + 4)
                link(dve.reciprocal(dst, deg[:, 3, :]), start + 5)

            def add_scaled(zi, bank, block0, inv):
                dve.wait_ge(z_ready, zi + 1)
                if not (isinstance(zi, int) and zi == 0):
                    dve.wait_ge(z_free, zi)
                for b in range(GB):
                    last = dve.scalar_tensor_tensor(out=x_sb[:, ds(block0 + b, 1), :],
                                                    in0=row_ps[bank][:, b * D:(b + 1) * D].rearrange("p (a f) -> p a f", a=1),
                                                    scalar=inv[:, ds(block0 + b, 1)],
                                                    in1=x_sb[:, ds(block0 + b, 1), :],
                                                    op0=ALU.mult, op1=ALU.add)
                last.then_inc(z_free, 1)

            def column_degrees(c, half):
                inverse_degree(inv_col[:, ds(CB * c + GB * half, GB)],
                               col_part[:, ds(CB * c + GB * half, GB), :], DEG_COL * c + 5 * half)

            def group_out(g):
                dve.wait_ge(nat_hi_done, ((NCH - 1) * NG + g + 1) * GB)
                inverse_degree(inv_row[:, GB * g:GB * g + GB], row_part[:, GB * g:GB * g + GB, :],
                               (NCH - 1) * DEG_COL + g * DEG_ROW + (DEG_COL if g == NG - 1 else 0))
                add_scaled(Z_ROW + g, g % 2, GB * g, inv_row)

            def sweep0(c, first, last):
                for g in range(NG):
                    for k in range(CB):
                        turn_out(c, g, k)
                        if first and (g, k) in FIRST_STATS:
                            first_stats(FIRST_STATS.index((g, k)) + 1)
                        if first and (g, k) in FIRST_AFFINE:
                            first_affine(FIRST_AFFINE.index((g, k)) + 1)
                        if first and g == 0 and k in (0, 1, 4, 5):
                            load_first_hc(k if k < 2 else k - 2)
                        if k == 3:
                            if g >= 1:
                                row_out(c, g - 1)
                            elif not first:
                                row_out(c - 1, NG - 1)
                        if not first and g == 0 and k in (4, 5):
                            column_degrees(c - 1, k - 4)
                        if not first and (g, k) in ((0, 7), (1, 1)):
                            half = g
                            add_scaled(2 * (c - 1) + half, 1, CB * (c - 1) + GB * half, inv_col)
                        if last and g >= 2 and k == 1:
                            dve.wait_ge(z_free, Z_ROW + g - 1)
                            ln_stats(0, g - 2)
                        if last and g >= 2 and k == 5:
                            ln_affine(0, g - 2)
                        if last and g >= 1 and k == 7:
                            group_out(g - 1)

            first_stats(0)
            first_affine(0)
            dve.wait_ge(acc_clear, 1)
            sweep0(0, True, False)
            with dve.Fori(1, NCH - 1) as c:
                sweep0(c, False, False)
            sweep0(NCH - 1, False, True)

            def finish_sweep0(s):
                if s == 0:
                    row_out(NCH - 1, NG - 1)
                if s in (1, 2):
                    half = s - 1
                    inverse_degree(inv_col[:, NB - CB + GB * half:NB - CB + GB * half + GB],
                                   col_part[:, NB - CB + GB * half:NB - CB + GB * half + GB, :],
                                   (NCH - 1) * DEG_COL + (NG - 1) * DEG_ROW + 5 * half)
                if s == 3:
                    group_out(NG - 1)
                if s in (4, 6):
                    half = s // 2 - 2
                    add_scaled(Z0 - 2 + half, half, NB - CB + GB * half, inv_col)
                for half, q in enumerate((NG - 2, NG - 1)):
                    at_stats, _, at_affine, at_norm, _ = LAST_TWO[half]
                    if s == at_stats:
                        dve.wait_ge(z_free, Z0 - 1 + half)
                        ln_stats(0, q)
                    if s == at_affine:
                        ln_affine(0, q)
                    if s == at_norm:
                        ln_apply(0, q)
                if s == 14:
                    dve.tensor_reduce(deg_sum[:, :], row_part[:, :, :], AX_X, ALU.add).then_inc(deg_step, 1)
                    dve.wait_ge(deg_step, DEG_ALL - 1)
                    dve.tensor_scalar(d_isqrt[:, :], deg_sum[:, :], 1.0, None, ALU.add).then_inc(deg_step, 1)
                if s == 15:
                    dve.wait_ge(dsq_ready, 1)
                    dve.reciprocal(d_isqrt[:, :], d_isqrt[:, :]).then_inc(dsq_ready, 1)
                    dve.wait_ge(dsq_ready, 2)

            def z_out(sweep, q, par):
                g = (sweep - 1) * NG + q
                bias = b_sb[:, B_OF[sweep]:B_OF[sweep] + 1, :].to_broadcast([P, GB, D])
                dve.wait_ge(z_ready, Z0 + g + 1)
                z4 = z_ps[par][:, :].rearrange("p (b f) -> p b f", b=GB)
                zt4 = zt[:, :].rearrange("p (b f) -> p b f", b=GB)
                if sweep in (1, 2):
                    if sweep == 1 and not (isinstance(q, int) and q == 0):
                        dve.wait_ge(act_ready, SPLIT_BEFORE[1] + q)
                    if sweep == 2 and isinstance(q, int) and q == 0:
                        dve.wait_ge(act_ready, SPLIT_BEFORE[1] + NG)
                    dve.tensor_tensor(zt4, z4, bias, ALU.add).then_inc(zt_ready, 1)
                else:
                    for b in range(GB):
                        last = dve.scalar_tensor_tensor(out=zt[:, b * D:(b + 1) * D], in0=z_ps[par][:, b * D:(b + 1) * D],
                                                        scalar=d_isqrt[:, ds(GB * q + b, 1)],
                                                        in1=b_sb[:, B_OF[sweep], :], op0=ALU.mult, op1=ALU.add)
                    last.then_inc(zt_ready, 1)
                    dve.wait_ge(zt_ready, 2 + ZT_BEFORE[sweep] + q + 1)
                    dve.scalar_tensor_tensor(out=x_sb[:, ds(GB * q, GB), :], in0=zt4, scalar=0.0,
                                             in1=x_sb[:, ds(GB * q, GB), :], op0=ALU.max, op1=ALU.add)\
                       .then_inc(x_upd, 1)

            def group(sweep, q, odd):
                ps, pq = before(sweep, q)
                for s in range(NS):
                    sidx = ((sweep - 1) * NG + q) * NS + s
                    if s not in POOL_LO:
                        dve.wait_ge(sub_hi, sidx + 1)
                        dve.tensor_tensor(sub(a_lo, s), sub_raw(sweep, q, s), sub(a_hi, s).bitcast(F32), ALU.subtract)\
                           .then_inc(sub_lo, 2 if s - 1 in POOL_LO else 1)
                    if ps == 0:
                        finish_sweep0(s)
                        continue
                    if s == AT_Z:
                        z_out(ps, pq, 1 - odd)
                    if s == AT_STATS[ps]:
                        if ps == 2:
                            x_plus_silu(pq)
                        dve.wait_ge(x_upd, XUPD_BEFORE[ps] + pq + 1)
                        ln_stats(ps, pq)
                    if s == AT_AFFINE[ps]:
                        ln_affine(ps, pq)
                    if s == AT_NORM[ps]:
                        ln_apply(ps, pq)

            def x_plus_silu(q):
                dve.wait_ge(silu_ready, q + 1)
                zt4 = zt[:, :].rearrange("p (b f) -> p b f", b=GB)
                dve.tensor_tensor(x_sb[:, ds(GB * q, GB), :], zt4, x_sb[:, ds(GB * q, GB), :], ALU.add)\
                   .then_inc(x_upd, 1)

            for sweep in range(1, SWEEPS + 1):
                run_groups(dve, sweep, group)
            z_out(SWEEPS, NG - 1, 1)

        @block.tensor
        def _(pe):
            pe.wait_ge(ident_made, 3)

            def split_products(ps, hi_w, lo_w, hi_a, lo_a, start, stop):
                pe.matmul(ps, hi_w, hi_a, start=start, stop=False)
                pe.matmul(ps, lo_w, hi_a, start=False, stop=False)
                return pe.matmul(ps, hi_w, lo_a, start=False, stop=stop)

            def weight_product(ps, src, w):
                for b in range(GB):
                    last = pe.matmul(ps[:, b * D:(b + 1) * D], src[:, b * P:(b + 1) * P], w_sb[:, w, :],
                                     start=True, stop=True)
                last.then_inc(z_ready, 1)

            LEAD = 3

            def turn(c, g, k):
                s = (c * NG + g) * CB + k
                if k == 0:
                    for a in range(GB):
                        pe.wait_ge(nat_in[4 * (g % 2) + a], 16 * (c * (NG // 2) + g // 2) + 16)
                if not (isinstance(s, int) and s < 4):
                    pe.wait_ge(at_lo_done, s - 3)
                for a in range(GB):
                    last = pe.transpose(turn_ps[k % 4][:, a * P:(a + 1) * P], nat_raw(g, a)[:, k * P:(k + 1) * P],
                                        ident[:, :])
                last.then_inc(turned, 1)

            def col_product(c, g, k):
                a, half = k // 2, k % 2
                n = (c * NG + g) * GB + a
                if isinstance(c, int) and c == 0 and k == 0:
                    pe.wait_ge(h_ready, g + 1)
                if g == 0 and k == 0:
                    pe.wait_ge(col_free, c + 1)
                if half == 0:
                    pe.wait_ge(nat_lo_done, n + 1)
                cols = slice(half * GW, (half + 1) * GW)
                last = split_products(col_ps[half][:, :], h_hi[0][:, GB * g + a, :], h_lo[0][:, GB * g + a, :],
                                      nat(a_hi, a)[:, cols], nat(a_lo, a)[:, cols],
                                      g == 0 and a == 0, g == NG - 1 and a == GB - 1)
                if half == 1:
                    last.then_inc(nat_free, 1)

            def row_product(c, g, k):
                s = (c * NG + g) * CB + k
                if k == 0:
                    pe.wait_ge(row_free, c * NG + g + 1)
                if g == 0 and k % 2 == 0:
                    pe.wait_ge(hc_ready, c * CB + k + 2)
                pe.wait_ge(at_lo_done, s + 1)
                last = split_products(row_ps[g % 2][:, :], hc_hi[:, k, :], hc_lo[:, k, :],
                                      atb(a_hi, k), atb(a_lo, k), k == 0, k == CB - 1)
                last.then_inc(at_free, 1)

            def row_weights(g):
                pe.wait_ge(row_free, 2 + (NCH - 1) * NG + g + 1)
                weight_product(row_ps[g % 2], acc[:, g * GW:(g + 1) * GW], 0)

            def sweep0(c, first, last):
                for g in range(NG):
                    for k in range(CB):
                        ahead = g * CB + k + LEAD
                        if not (last and ahead >= NG * CB):
                            turn(c + ahead // (NG * CB), ahead // CB % NG, ahead % CB)
                        col_product(c, g, k)
                        if last and g >= 2 and k == 0:
                            pe.wait_ge(z_free, Z_ROW + g - 1)
                        if not first and g == 1 and k == 0:
                            pe.wait_ge(z_free, 2 * c)
                        row_product(c, g, k)
                        if last and g >= 1 and k == 3:
                            row_weights(g - 1)
                        if not first and g == 0 and k in (3, 6):
                            half = k // 6
                            if half == 0:
                                pe.wait_ge(row_free, 2 + c * NG)
                                pe.wait_ge(col_free, c + 1)
                            else:
                                pe.wait_ge(z_free, 2 * c - 1)
                            weight_product(row_ps[1], prod_t[:, half, :], 1)

            for k in range(LEAD):
                turn(0, 0, k)
            sweep0(0, True, False)
            pe.wait_ge(const_in, 16 * 8)
            with pe.Fori(1, NCH - 1) as c:
                sweep0(c, False, False)
            sweep0(NCH - 1, False, True)

            def finish_sweep0(s):
                if s == 0:
                    row_weights(NG - 1)
                if s == 1:
                    pe.wait_ge(col_free, NCH + 1)
                    pe.wait_ge(z_free, Z0 - 3)
                    weight_product(row_ps[0], prod_t[:, 0, :], 1)
                if s == 3:
                    pe.wait_ge(z_free, Z0 - 2)
                    weight_product(row_ps[1], prod_t[:, 1, :], 1)

            def group(sweep, q, odd):
                s_in = SET_OF[sweep - 1]
                hi, lo = h_hi[s_in], h_lo[s_in]
                ps, pq = before(sweep, q)
                gidx = (sweep - 1) * NG + q
                bank = prod_ps[odd][:, :]
                first_group = isinstance(q, int) and q == 0
                if sweep == 1 and first_group:
                    pe.wait_ge(at_lo_done, STEPS)
                pe.wait_ge(prod_free, gidx + 1)
                for s in range(NS):
                    sidx = gidx * NS + s
                    if first_group and s % 2 == 0:
                        pe.wait_ge(h_ready, SPLIT_BEFORE[sweep - 1] + s // 2 + 1)
                    pe.wait_ge(sub_hi, sidx + 1)
                    for b in range(SB2):
                        cols = slice(b * GW, (b + 1) * GW)
                        pe.matmul(bank, hi[:, SB2 * s + b, :], sub(a_hi, s)[:, cols], start=(s == 0 and b == 0), stop=False)
                        pe.matmul(bank, lo[:, SB2 * s + b, :], sub(a_hi, s)[:, cols], start=False, stop=False)
                    if s in POOL_LO:
                        pe.wait_ge(sub_lo_pool, gidx * NS + POOL_LO[s])
                    else:
                        pe.wait_ge(sub_lo, sidx + 1)
                    for b in range(SB2):
                        cols = slice(b * GW, (b + 1) * GW)
                        last = pe.matmul(bank, hi[:, SB2 * s + b, :], sub(a_lo, s)[:, cols], start=False,
                                         stop=(s == NS - 1 and b == SB2 - 1))
                    last.then_inc(sub_used, 1)
                    if s == NS - 3 and sweep >= 3:
                        identity_product(sweep, q, bank)
                    if ps == 0:
                        finish_sweep0(s)
                    if s == AT_WEIGHTS and ps > 0:
                        finish(ps, pq, 1 - odd)

            def identity_product(sweep, q, bank):
                pe.wait_ge(hd_ready, 2 * ((sweep - 3) * NG + q) + 2)
                for b in range(GB):
                    for part in (hd_hi, hd_lo):
                        pe.matmul(bank[:, b * P:(b + 1) * P], part[:, b, :], ident_r[:, :], start=False, stop=False,
                                  skip_group_check=True)

            def finish(sweep, q, par):
                g = (sweep - 1) * NG + q
                pe.wait_ge(prod_free, 2 + g + 1)
                pe.wait_ge(zt_ready, g + 1)
                weight_product(z_ps[par], prod_t[:, par, :], W_OF[sweep])

            for sweep in range(1, SWEEPS + 1):
                run_groups(pe, sweep, group)
            finish(SWEEPS, NG - 1, 1)


_INS = ['x', 'adj', 'L0_gnn_W_in', 'L0_gnn_W_out', 'L1_gnn_W', 'L1_gnn_b', 'L2_gnn_W', 'L2_gnn_b',
        'L3_gnn_W', 'L3_gnn_b']
_OUTS = [((4096, 128), 'float32')]


def kernel(**inputs):
    import numpy as _np
    import concourse.bacc as _bacc
    from concourse import mybir as _mybir
    from concourse.bass_utils import run_bass_kernel_spmd as _run

    nc = _bacc.Bacc("TRN2", target_bir_lowering=False, num_devices=1)
    arrays, args = {}, []
    for name in _INS:
        a = _np.ascontiguousarray(inputs[name])
        arrays[f"in_{name}_dram"] = a
        args.append(nc.dram_tensor(f"in_{name}_dram", a.shape, _mybir.dt.from_np(a.dtype), kind="ExternalInput").ap())
    for i, (shape, dtype) in enumerate(_OUTS):
        dt = _mybir.dt.from_np(_np.dtype(dtype))
        args.append(nc.dram_tensor(f"out_{i}_dram", shape, dt, kind="ExternalOutput").ap())
    build_gnn_stack(nc, *args)
    r = _run(nc, [arrays], core_ids=[0])
    got = tuple(r.results[0][f"out_{i}_dram"] for i in range(len(_OUTS)))
    return got[0]
```
